# Optimizing a Trainium2 kernel written in Bass

```python
import numpy as np
import jax
import jax.numpy as jnp

def _softmax(x, axis=-1):
    return jax.nn.softmax(x, axis=axis)

def _gelu(x):
    return jax.nn.gelu(x, approximate=True)

def _silu(x):
    return jax.nn.silu(x)

def _sigmoid(x):
    return jax.nn.sigmoid(x)

def _layernorm(x, axis=-1, eps=1e-05):
    m = jnp.mean(x, axis=axis, keepdims=True)
    v = jnp.var(x, axis=axis, keepdims=True)
    return (x - m) / jnp.sqrt(v + eps)

def _scatter_add(tgt, idx, src, axis=0):
    return tgt.at[idx].add(src)

def _segment_sum(src, seg, n):
    return jax.ops.segment_sum(src, seg, n)
kernel_name = 'mk_adaln_ffn_d2_seqx_r8_d4e09d'

def setup_inputs(seed: int=0):
    np.random.seed(seed)
    _w = jnp.asarray

    def _rec_inputs():
        import jax
        import jax.numpy as jnp
        _rk = jax.random.key(seed)
        x = -1.394e-06 + 0.9999 * jax.random.normal(jax.random.fold_in(_rk, 1), (4, 256, 256), jnp.float32)
        _lenS = 256 - jax.random.randint(jax.random.fold_in(_rk, 7), (4,), 0, max(1, 256 // 4) + 1, jnp.int32)
        _lenS2 = 256 - jax.random.randint(jax.random.fold_in(_rk, 8), (4,), 0, max(1, 256 // 4) + 1, jnp.int32)
        cond_2048 = -0.00499425 + 1.0058 * jax.random.normal(jax.random.fold_in(_rk, 11), (4, 256), jnp.float32)
        return (x, cond_2048)
    x, cond_2048 = _rec_inputs()

    def _L0_cond_setup():
        import jax, jax.numpy as jnp
        import numpy as np
        B, T, D = (16, 128, 256)
        key = jax.random.key(seed)
        k0, k1, k2, k3 = jax.random.split(key, 4)
        scale = 1.0 / np.sqrt(D)
        return {'initial_state': jax.random.normal(k0, (B, D), jnp.float32), 'inputs': jax.random.normal(k1, (B, T, D), jnp.float32), 'W_ih': jax.random.normal(k2, (D, 3 * D), jnp.float32) * scale, 'W_hh': jax.random.normal(k3, (D, 3 * D), jnp.float32) * scale, 'b_ih': jnp.zeros((3 * D,), jnp.float32), 'b_hh': jnp.zeros((3 * D,), jnp.float32)}
    _L0_cond_all = _L0_cond_setup()
    _L0_cond_in = {k: v for k, v in _L0_cond_all.items() if k in ('W_ih', 'W_hh', 'b_ih', 'b_hh')}
    del _L0_cond_all

    def _L0_ffn_setup():
        import jax, jax.numpy as jnp
        import numpy as np
        B, S, D, I, E, K = (4, 128, 256, 128, 8, 2)
        key = jax.random.key(seed)
        ks = jax.random.split(key, 7)

        def w(k, shape, fan_in):
            return jax.random.normal(k, shape, dtype=jnp.float32) * fan_in ** (-0.5)
        return {'hidden_states': jax.random.normal(ks[0], (B, S, D), dtype=jnp.float32), 'router_w': w(ks[1], (D, E), D), 'gate_up_w': w(ks[2], (E, D, 2 * I), D), 'down_w': w(ks[3], (E, I, D), I), 'shared_gate_w': w(ks[4], (D, I), D), 'shared_up_w': w(ks[5], (D, I), D), 'shared_down_w': w(ks[6], (I, D), I)}
    _L0_ffn_all = _L0_ffn_setup()
    _L0_ffn_in = {k: v for k, v in _L0_ffn_all.items() if k in ('router_w', 'gate_up_w', 'down_w', 'shared_gate_w', 'shared_up_w', 'shared_down_w')}
    del _L0_ffn_all

    def _L1_cond_setup():
        import jax, jax.numpy as jnp
        import numpy as np
        key = jax.random.key(seed)
        k1, k2, k3 = jax.random.split(key, 3)
        B, L, D, K = (4, 512, 256, 4)
        x = jax.random.normal(k1, (B, L, D), dtype=jnp.float32)
        w = jax.random.normal(k2, (K, 1, D), dtype=jnp.float32) * 0.1
        b = jax.random.normal(k3, (D,), dtype=jnp.float32) * 0.1
        return {'x': x, 'w': w, 'b': b}
    _L1_cond_all = _L1_cond_setup()
    _L1_cond_in = {k: v for k, v in _L1_cond_all.items() if k in ('b',)}
    del _L1_cond_all

    def _L1_ffn_setup():
        import jax, jax.numpy as jnp
        import numpy as np
        H = 256
        E = 8
        K = 2
        I = 16
        key = jax.random.key(seed)
        k1, k2, k3, k4 = jax.random.split(key, 4)
        B, T = (2, 512)
        x = jax.random.normal(k1, (B, T, H), dtype=jnp.float32)
        router_w = jax.random.normal(k2, (E, H), dtype=jnp.float32) / np.sqrt(H)
        down_w = jax.random.normal(k3, (E, I, H), dtype=jnp.float32) / np.sqrt(H)
        up_w = jax.random.normal(k4, (E, H, I), dtype=jnp.float32) / np.sqrt(I)
        return {'x': x, 'router_w': router_w, 'down_w': down_w, 'up_w': up_w}
    _L1_ffn_all = _L1_ffn_setup()
    _L1_ffn_in = {k: v for k, v in _L1_ffn_all.items() if k in ('router_w', 'down_w', 'up_w')}
    del _L1_ffn_all
    return {'x': x, 'cond_2048': cond_2048, 'L0_cond_W_ih': _L0_cond_in['W_ih'], 'L0_cond_W_hh': _L0_cond_in['W_hh'], 'L0_cond_b_ih': _L0_cond_in['b_ih'], 'L0_cond_b_hh': _L0_cond_in['b_hh'], 'L0_ffn_router_w': _L0_ffn_in['router_w'], 'L0_ffn_gate_up_w': _L0_ffn_in['gate_up_w'], 'L0_ffn_down_w': _L0_ffn_in['down_w'], 'L0_ffn_shared_gate_w': _L0_ffn_in['shared_gate_w'], 'L0_ffn_shared_up_w': _L0_ffn_in['shared_up_w'], 'L0_ffn_shared_down_w': _L0_ffn_in['shared_down_w'], 'L1_cond_b': _L1_cond_in['b'], 'L1_ffn_router_w': _L1_ffn_in['router_w'], 'L1_ffn_down_w': _L1_ffn_in['down_w'], 'L1_ffn_up_w': _L1_ffn_in['up_w']}

def reference(x, cond_2048, L0_cond_W_ih, L0_cond_W_hh, L0_cond_b_ih, L0_cond_b_hh, L0_ffn_router_w, L0_ffn_gate_up_w, L0_ffn_down_w, L0_ffn_shared_gate_w, L0_ffn_shared_up_w, L0_ffn_shared_down_w, L1_cond_b, L1_ffn_router_w, L1_ffn_down_w, L1_ffn_up_w):
    import jax
    import jax.numpy as jnp

    def _L0_cond_ref(initial_state, inputs, W_ih, W_hh, b_ih, b_hh):
        import jax, jax.numpy as jnp
        import numpy as np
        B, T, D = (16, 128, 256)
        "ScanOverTime(GRU cell): sequential per-timestep module call with\n            dict-state passing; merge_dict_trees stacks the per-step\n            'state_predicted' tensors along axis=1 -> [B, T, D]."

        def cell(h, x):
            gi = x @ W_ih + b_ih
            gh = h @ W_hh + b_hh
            i_r, i_z, i_n = jnp.split(gi, 3, axis=-1)
            h_r, h_z, h_n = jnp.split(gh, 3, axis=-1)
            r = jax.nn.sigmoid(i_r + h_r)
            z = jax.nn.sigmoid(i_z + h_z)
            n = jnp.tanh(i_n + r * h_n)
            h_new = (1.0 - z) * n + z * h
            return (h_new, h_new)
        xs = jnp.swapaxes(inputs, 0, 1)
        _, hs = jax.lax.scan(cell, initial_state, xs)
        return jnp.swapaxes(hs, 0, 1)

    def _L0_ffn_ref(hidden_states, router_w, gate_up_w, down_w, shared_gate_w, shared_up_w, shared_down_w):
        import jax, jax.numpy as jnp
        import numpy as np
        B, S, D, I, E, K = (4, 128, 256, 128, 8, 2)
        Bb, Ss, Dd = hidden_states.shape
        x = hidden_states.reshape(-1, Dd)
        T = x.shape[0]
        shared = jax.nn.silu(x @ shared_gate_w) * (x @ shared_up_w) @ shared_down_w
        logits = x @ router_w
        top_val, top_idx = jax.lax.top_k(logits, K)
        probs = jnp.zeros_like(logits).at[jnp.arange(T)[:, None], top_idx].set(jax.nn.sigmoid(top_val))
        xin = probs.T[:, :, None] * x[None]
        gu = jnp.einsum('etd,edf->etf', xin, gate_up_w)
        gate, up = jnp.split(gu, 2, axis=-1)
        h = jax.nn.silu(gate) * up
        expert_out = jnp.einsum('eti,eid->etd', h, down_w)
        combined = shared + expert_out.sum(axis=0)
        return combined.reshape(Bb, Ss, Dd)

    def _L1_cond_ref(x, w, b):
        import jax, jax.numpy as jnp
        import numpy as np
        'Depthwise causal conv1d, channel-last.\n            x: (B, L, D); w: (K, 1, D); b: (D,). Returns (B, L, D).\n            Matches torch: Conv1d(D, D, K, groups=D, padding=K-1)(x.T)[..., :L].T\n            which is exactly a causal conv (left pad K-1, trim to L).\n            '
        K = w.shape[0]
        D = x.shape[-1]
        y = jax.lax.conv_general_dilated(x, w, window_strides=(1,), padding=[(K - 1, 0)], feature_group_count=D, dimension_numbers=('NWC', 'WIO', 'NWC'))
        return y + b

    def _L1_ffn_ref(x, router_w, down_w, up_w):
        import jax, jax.numpy as jnp
        import numpy as np
        H = 256
        E = 8
        K = 2
        I = 16
        logits = jnp.einsum('bth,eh->bte', x, router_w)
        weights = jax.nn.softmax(logits, axis=-1)
        top_w, top_idx = jax.lax.top_k(weights, K)
        topk_mask = jnp.sum(jax.nn.one_hot(top_idx, E, dtype=x.dtype), axis=-2)
        gate = weights * topk_mask
        h = jnp.einsum('bth,eih->beti', x, down_w)
        a = jax.nn.silu(h)
        expert_out = jnp.einsum('beti,ehi->beth', a, up_w)
        out = jnp.einsum('beth,bte->bth', expert_out, gate)
        return out
    x = x + _L0_ffn_ref(_L0_cond_ref(cond_2048, x, L0_cond_W_ih, L0_cond_W_hh, L0_cond_b_ih, L0_cond_b_hh), L0_ffn_router_w, L0_ffn_gate_up_w, L0_ffn_down_w, L0_ffn_shared_gate_w, L0_ffn_shared_up_w, L0_ffn_shared_down_w)
    x = x + _L1_ffn_ref(_L1_cond_ref(x, cond_2048[:, None, :], L1_cond_b), L1_ffn_router_w, L1_ffn_down_w, L1_ffn_up_w)
    return x

_drawn_inputs = setup_inputs


def setup_inputs(seed=0):
    import zlib

    import numpy as np

    out = dict(_drawn_inputs(seed))
    spreads = {'L0_cond_b_ih': (0.0, 0.1), 'L0_cond_b_hh': (0.0, 0.1)}
    factors = {}
    for name, (base, spread) in spreads.items():
        noise = np.random.default_rng([zlib.crc32(name.encode()), seed]).standard_normal(out[name].shape)
        drawn = base * np.exp(spread * noise) if base else spread * noise
        out[name] = jnp.asarray(drawn.astype(out[name].dtype))
    for name, factor in factors.items():
        out[name] = (out[name] * factor).astype(out[name].dtype)
    return out
```

```python
from contextlib import ExitStack

import concourse.bass as bass
from concourse import mybir

F32 = mybir.dt.float32
ALU = mybir.AluOpType
ACT = mybir.ActivationFunctionType
AX = mybir.AxisListType

P = 128
B = 4
D = 256
T = 256
HALVES = D // P
STEPS = P // B
CHUNKS = T // STEPS
G3 = 3 * D
HB = HALVES * B
QUADS = 4
QF = P // QUADS
E0, I0 = 8, 128
E1, I1 = 8, 16
UNITS = E0 + 1
TAPS = 4
CARRY = (TAPS - 1) * B


def build(nc, x_c, h0_c, w_ih_d, w_hh_d, b_ih_row, b_hh_row, b_ih_c, b_hh_c, r0_d, gu_d, dn_d, sg_d, su_d, sd_d,
          conv_b_c, r1_d, d1_d, u1_d, out_c):
    with ExitStack() as ctx:
        def sb(name, shape, dt=F32):
            return ctx.enter_context(nc.sbuf_tensor(name, shape, dt))

        def bank(name, shape):
            return ctx.enter_context(nc.psum_tensor(name, shape, F32))

        def sem(name):
            return ctx.enter_context(nc.semaphore(name))

        w_ih = sb("w_ih", [P, HALVES, G3])
        w_hh = sb("w_hh", [P, HALVES, G3])
        gate_up = sb("gate_up", [P, UNITS, HALVES, 2 * I0])
        down = sb("down", [P, UNITS, D])
        router0 = sb("router0", [P, HALVES, E0])
        proj1 = sb("proj1", [P, HALVES, E1 * I1 + E1])
        up1 = sb("up1", [P, D])
        ident = sb("ident", [P, P])
        ones = sb("ones", [P, HALVES, P])
        bias_rows = sb("bias_rows", [1, 2, G3])
        rz_bias = sb("rz_bias", [1, 2 * D])
        b_in = sb("b_in", [P, HALVES])
        neg_b_in = sb("neg_b_in", [P, HALVES])
        b_hn = sb("b_hn", [P, HALVES])
        neg_b_hn = sb("neg_b_hn", [P, HALVES, B])
        cond = sb("cond", [P, HALVES, B])
        conv_b = sb("conv_b", [P, HALVES])
        table_warm = sb("table_warm", [P, 1])
        before = sb("before", [P, E0, E0])

        hid = [sb(f"hid{i}", [P, 3 * HB + 2]) for i in range(2)]
        turned_r = sb("turned_r", [P, HALVES * QF])
        turned_hn = sb("turned_hn", [P, HALVES * QF])
        turned_z = sb("turned_z", [P, HALVES * QF])
        cand_mul = sb("cand_mul", [P, 3 * HB])
        cand_out = sb("cand_out", [P, 3 * HB])
        upd_mul = sb("upd_mul", [P, 3 * HB])
        cand_in = sb("cand_in", [P, STEPS, 3 * HB])
        gi_rz = sb("gi_rz", [P, 2 * D])
        hist = sb("hist", [P, HALVES, P])
        moe0_x = sb("moe0_x", [P, HALVES, P])

        x_pre = sb("x_pre", [P, HALVES, P])
        x_res = sb("x_res", [P, HALVES, P])
        x1 = sb("x1", [P, HALVES, CARRY + P])
        logits0 = sb("logits0", [P, E0])
        sig0 = sb("sig0", [P, E0])
        pairs = sb("pairs", [P, E0, 2, E0])
        rank = sb("rank", [P, E0])
        probs = sb("probs", [P, E0])
        sig_gate = sb("sig_gate", [P, I0])
        act_gate = sb("act_gate", [P, I0])
        hidden0 = sb("hidden0", [P, I0])
        hidden0_c = sb("hidden0_c", [P, P])
        y = sb("y", [P, HALVES, P])
        hx1 = sb("hx1", [P, E1 * I1 + E1])
        top1 = sb("top1", [P, 1])
        neg_top1 = sb("neg_top1", [P, 1])
        sig_up = sb("sig_up", [P, E1])
        sig_dn = sb("sig_dn", [P, E1])
        expd = sb("expd", [P, E1])
        total = sb("total", [P, 1])
        weights = sb("weights", [P, E1])
        gate1 = sb("gate1", [P, E1])
        sig_hx = sb("sig_hx", [P, E1 * I1])
        act1 = sb("act1", [P, E1 * I1])
        gated1 = sb("gated1", [P, E1 * I1])
        gated1_c = sb("gated1_c", [P, P])
        out_sb = sb("out_sb", [P, HALVES, P])

        ps_r = bank("ps_r", [P, 512])
        ps_hn = bank("ps_hn", [P, 512])
        ps_z = bank("ps_z", [P, 512])
        ps_gi = bank("ps_gi", [P, 512])
        ps_gu = bank("ps_gu", [P, 512])
        ps_t = bank("ps_t", [P, 512])
        ps_moe0 = bank("ps_moe0", [P, 512])
        ps_moe1 = bank("ps_moe1", [P, 512])

        loaded_gru = sem("loaded_gru")
        loaded_in = sem("loaded_in")
        loaded_small = sem("loaded_small")
        loaded_moe = sem("loaded_moe")
        pool_const = sem("pool_const")
        cleared = sem("cleared")
        biases_ready = sem("biases_ready")
        masks_ready = sem("masks_ready")
        x_pre_loaded = sem("x_pre_loaded")
        x_res_loaded = sem("x_res_loaded")
        stored = sem("stored")
        h_ready = sem("h_ready")
        r_summed = sem("r_summed")
        hn_summed = sem("hn_summed")
        z_summed = sem("z_summed")
        r_turned = sem("r_turned")
        hn_turned = sem("hn_turned")
        hn_placed = sem("hn_placed")
        z_turned = sem("z_turned")
        r_ready = sem("r_ready")
        z_ready = sem("z_ready")
        arg_ready = sem("arg_ready")
        n_ready = sem("n_ready")
        hist_kept = sem("hist_kept")
        gi_used = sem("gi_used")
        gi_summed = sem("gi_summed")
        gi_ready = sem("gi_ready")
        in_summed = sem("in_summed")
        in_ready = sem("in_ready")
        moe0_x_ready = sem("moe0_x_ready")
        logits0_summed = sem("logits0_summed")
        logits0_ready = sem("logits0_ready")
        sig0_ready = sem("sig0_ready")
        rank0_step = sem("rank0_step")
        gu_summed = sem("gu_summed")
        sig_gate_ready = sem("sig_gate_ready")
        act_gate_ready = sem("act_gate_ready")
        hidden0_ready = sem("hidden0_ready")
        hidden0_turned = sem("hidden0_turned")
        hidden0_c_ready = sem("hidden0_c_ready")
        down_summed = sem("down_summed")
        x1_ready = sem("x1_ready")
        conv_step = sem("conv_step")
        proj1_summed = sem("proj1_summed")
        hx1_ready = sem("hx1_ready")
        top1_ready = sem("top1_ready")
        exp_ready = sem("exp_ready")
        soft_step = sem("soft_step")
        sig_hx_ready = sem("sig_hx_ready")
        act1_ready = sem("act1_ready")
        gated1_ready = sem("gated1_ready")
        gated1_turned = sem("gated1_turned")
        gated1_c_ready = sem("gated1_c_ready")
        moe1_summed = sem("moe1_summed")
        out_ready = sem("out_ready")
        carried = sem("carried")

        SMALL_LOADS, MOE_LOADS = 6, 9
        CLEARS, BIASES, POOL_CONSTS = 9, 2 + B, 5
        CONV_OPS = HALVES * TAPS
        RANK_OPS = 4
        SOFT_OPS = 9

        def gate_cols(w, k, gate, quad):
            cols = w[:, k, gate * D:(gate + 1) * D] if k is not None else w[:, gate * D:(gate + 1) * D]
            return cols.rearrange("p (c q f) -> p c q f", c=HALVES, q=QUADS)[:, :, quad, :]

        def gate_out(ps, quad):
            return ps[QF * quad:QF * quad + B, 0:HALVES * QF].rearrange("p (c f) -> p c f", c=HALVES)

        def hid_cols(i, k=None):
            trip = hid[i % 2][:, 2:2 + 3 * HB].rearrange("p (c b three) -> p c b three", c=HALVES, b=B)
            return trip[:, :, :, 0] if k is None else trip[:, k, :, 0]

        def third(buf, i):
            return buf.rearrange("p (c b three) -> p c b three", c=HALVES, b=B)[:, :, :, i]

        def turned(buf):
            return buf[:, :].rearrange("p (c f) -> p c f", c=HALVES)[:, :, 0:B]

        def runs_after(n, least):
            return not isinstance(n, int) or n >= least

        FIRST_LOOP, LAST_LOOP = 2, CHUNKS - 2

        def iterations(eng, run):
            run(0, gru=True, pre=True, moe0=False, moe1=False)
            run(1, gru=True, pre=True, moe0=True, moe1=False)
            with eng.Fori(FIRST_LOOP, LAST_LOOP + 1) as c:
                run(c, gru=True, pre=True, moe0=True, moe1=True)
            run(CHUNKS - 1, gru=True, pre=False, moe0=True, moe1=True)
            run(CHUNKS, gru=False, pre=False, moe0=True, moe1=True)
            run(CHUNKS + 1, gru=False, pre=False, moe0=False, moe1=True)

        def unit_of(s, at):
            u, rest = divmod(s - at, 3)
            return u if rest == 0 and 0 <= u < UNITS else None

        block = ctx.enter_context(nc.Block())

        @block.sync
        def _(sp):
            sp.dma_start(x_pre[:, :, :], x_c[0].rearrange("p (c t) -> p c t", c=HALVES)).then_inc(x_pre_loaded, 16)
            sp.dma_start(w_ih[:, :, :], w_ih_d).then_inc(loaded_in, 16)
            sp.dma_start(w_hh[:, :, :], w_hh_d).then_inc(loaded_gru, 16)
            sp.dma_start(gate_up[:, 1:UNITS, :, :], gu_d).then_inc(loaded_moe, 16)
            sp.dma_start(down[:, 1:UNITS, :], dn_d).then_inc(loaded_moe, 16)

            def run(c, gru, pre, moe0, moe1):
                if pre:
                    sp.wait_ge(in_summed, c + 1)
                    sp.dma_start(x_pre[:, :, :], x_c[c + 1].rearrange("p (c t) -> p c t", c=HALVES))\
                      .then_inc(x_pre_loaded, 16)
                if moe0:
                    if runs_after(c, 2):
                        sp.wait_ge(x1_ready, c - 1)
                    sp.dma_start(x_res[:, :, :], x_c[c - 1].rearrange("p (c t) -> p c t", c=HALVES))\
                      .then_inc(x_res_loaded, 16)
                if moe1:
                    sp.wait_ge(out_ready, c - 1)
                    sp.dma_start(out_c[c - 2].rearrange("p (c t) -> p c t", c=HALVES), out_sb[:, :, :])\
                      .then_inc(stored, 16)

            iterations(sp, run)
            sp.wait_ge(stored, 16 * CHUNKS)

        @block.gpsimd
        def _(pool):
            nc.gpsimd.memset(ident[:, :], 0.0).then_inc(pool_const, 1)
            nc.gpsimd.memset(before[:, :, :], 1.0).then_inc(pool_const, 1)
            nc.gpsimd.memset(ones[:, :, :], 1.0).then_inc(pool_const, 1)
            pool.wait_ge(pool_const, 3)
            nc.gpsimd.affine_select(out=ident[:, :], in_=ident[:, :], compare_op=ALU.not_equal, fill=1.0, base=0,
                                    pattern=[[-1, P]], channel_multiplier=1).then_inc(pool_const, 1)
            nc.gpsimd.affine_select(out=before[:, :, :], in_=before[:, :, :], compare_op=ALU.is_gt, fill=0.0, base=0,
                                    pattern=[[1, E0], [-1, E0]], channel_multiplier=0).then_inc(pool_const, 1)

            def run(c, gru, pre, moe0, moe1):
                if not gru:
                    return
                for s in range(STEPS):
                    pool.wait_ge(h_ready, STEPS * c + s + 2)
                    nc.gpsimd.tensor_tensor(hist[:, :, B * s:B * s + B], hid_cols(s + 1), ones[:, :, 0:B], ALU.mult)\
                      .then_inc(hist_kept, 1)
                if runs_after(c, 1):
                    pool.wait_ge(gu_summed, UNITS * c)
                pool.wait_ge(hist_kept, STEPS * (c + 1))
                nc.gpsimd.tensor_tensor(moe0_x[:, :, :], hist[:, :, :], ones[:, :, :], ALU.mult)\
                  .then_inc(moe0_x_ready, 1)
                pool.wait_ge(moe0_x_ready, c + 1)

            iterations(pool, run)

        @block.scalar
        def _(act):
            act.dma_start(cond[:, :, :], h0_c).then_inc(loaded_small, 16)
            act.dma_start(bias_rows[:, 0, :], b_ih_row).then_inc(loaded_small, 16)
            act.dma_start(bias_rows[:, 1, :], b_hh_row).then_inc(loaded_small, 16)
            act.dma_start(b_in[:, :], b_ih_c).then_inc(loaded_small, 16)
            act.dma_start(b_hn[:, :], b_hh_c).then_inc(loaded_small, 16)
            act.dma_start(conv_b[:, :], conv_b_c).then_inc(loaded_small, 16)
            act.dma_start(router0[:, :, :], r0_d).then_inc(loaded_moe, 16)
            act.dma_start(gate_up[:, 0, :, 0:I0], sg_d).then_inc(loaded_moe, 16)
            act.dma_start(gate_up[:, 0, :, I0:2 * I0], su_d).then_inc(loaded_moe, 16)
            act.dma_start(down[:, 0, :], sd_d).then_inc(loaded_moe, 16)
            act.dma_start(proj1[:, :, 0:E1 * I1], d1_d).then_inc(loaded_moe, 16)
            act.dma_start(proj1[:, :, E1 * I1:E1 * I1 + E1], r1_d).then_inc(loaded_moe, 16)
            act.dma_start(up1[:, :], u1_d).then_inc(loaded_moe, 16)

            def copy_gi(q):
                act.wait_ge(gi_summed, q + 1)
                if runs_after(q, 1):
                    act.wait_ge(gi_used, q)
                nc.scalar.activation(gi_rz[:, :], ps_gi[:, :], ACT.Copy).then_inc(gi_ready, 1)

            def place_in(q):
                act.wait_ge(in_summed, q + 1)
                for half in range(HALVES):
                    dst = cand_in[:, :, :].rearrange("p s (c b three) -> p s c b three", c=HALVES, b=B)
                    nc.scalar.activation(
                        dst[:, :, half, :, 1],
                        ps_moe1[:, half * P:(half + 1) * P].rearrange("p (s b) -> p s b", b=B),
                        ACT.Identity, bias=neg_b_in[:, half:half + 1], scale=-1.0).then_inc(in_ready, 1)

            act.wait_ge(biases_ready, BIASES)
            act.wait_ge(cleared, CLEARS)
            nc.scalar.activation(table_warm[:, :], neg_b_in[:, 0:1], ACT.Sigmoid)
            copy_gi(0)
            place_in(0)

            def gru_step(c, s):
                n = STEPS * c + s
                act.wait_ge(r_turned, n + 1)
                nc.scalar.activation(third(cand_mul[:, :], 1), turned(turned_r), ACT.Sigmoid).then_inc(r_ready, 1)
                act.wait_ge(arg_ready, n + 1)
                trip_in = cand_out[:, :].rearrange("p (j three) -> p j three", three=3)[:, :, 1:3]
                trip_out = hid[s % 2][:, 2:2 + 3 * HB].rearrange("p (j three) -> p j three", three=3)[:, :, 1:3]
                nc.scalar.activation(trip_out, trip_in, ACT.Tanh).then_inc(n_ready, 1)
                act.wait_ge(z_turned, n + 1)
                nc.scalar.activation(third(upd_mul[:, :], 2), turned(turned_z), ACT.Sigmoid).then_inc(z_ready, 1)

            def run(c, gru, pre, moe0, moe1):
                for s in range(STEPS):
                    if gru:
                        gru_step(c, s)
                    if moe0:
                        q = c - 1
                        if s == 2:
                            act.wait_ge(logits0_ready, q + 1)
                            nc.scalar.activation(sig0[:, :], logits0[:, :], ACT.Sigmoid).then_inc(sig0_ready, 1)
                        u = unit_of(s, 1)
                        if u is not None:
                            n = UNITS * q + u
                            act.wait_ge(gu_summed, n + 1)
                            if u == 0:
                                if runs_after(q, 1):
                                    act.wait_ge(hidden0_ready, n)
                                nc.scalar.activation(sig_gate[:, :], ps_gu[:, 0:I0], ACT.Sigmoid)\
                                  .then_inc(sig_gate_ready, 1)
                            else:
                                act.wait_ge(hidden0_ready, n)
                                if u == 1:
                                    act.wait_ge(rank0_step, RANK_OPS * (q + 1))
                                nc.scalar.activation(sig_gate[:, :], ps_gu[:, 0:I0], ACT.Sigmoid,
                                                     scale=probs[:, u - 1:u]).then_inc(sig_gate_ready, 1)
                        u = unit_of(s, 3)
                        if u is not None:
                            n = UNITS * q + u
                            act.wait_ge(hidden0_turned, n + 1)
                            if runs_after(n, 1):
                                act.wait_ge(down_summed, n)
                            nc.scalar.activation(hidden0_c[:, :], ps_t[:, 0:P], ACT.Copy).then_inc(hidden0_c_ready, 1)
                    if moe1:
                        q = c - 2
                        if s == 11:
                            act.wait_ge(top1_ready, 2 * (q + 1))
                            nc.scalar.activation(sig_up[:, :], hx1[:, E1 * I1:E1 * I1 + E1], ACT.Sigmoid,
                                                 bias=neg_top1[:, 0:1]).then_inc(exp_ready, 1)
                            nc.scalar.activation(sig_dn[:, :], hx1[:, E1 * I1:E1 * I1 + E1], ACT.Sigmoid,
                                                 bias=top1[:, 0:1], scale=-1.0).then_inc(exp_ready, 1)
                            nc.scalar.activation(sig_hx[:, :], hx1[:, 0:E1 * I1], ACT.Sigmoid).then_inc(sig_hx_ready, 1)
                        if s == 17:
                            act.wait_ge(gated1_turned, q + 1)
                            nc.scalar.activation(gated1_c[:, :], ps_moe1[:, D:D + P], ACT.Copy).then_inc(gated1_c_ready, 1)
                    if pre:
                        if s == STEPS - 2:
                            copy_gi(c + 1)
                        if s == STEPS - 1:
                            place_in(c + 1)

            iterations(act, run)

        @block.vector
        def _(dve):
            for part in (ps_r[:, 0:HALVES * QF], ps_hn[:, 0:HALVES * QF], ps_z[:, 0:HALVES * QF], cand_mul[:, :],
                         upd_mul[:, :], cand_in[:, :, :], hid[0][:, :], hid[1][:, :], x1[:, :, 0:CARRY]):
                nc.vector.memset(part, 0.0).then_inc(cleared, 1)
            dve.wait_ge(loaded_small, 16 * SMALL_LOADS)
            nc.vector.tensor_scalar(neg_b_in[:, :], b_in[:, :], -1.0, None, ALU.mult).then_inc(biases_ready, 1)
            nc.vector.tensor_tensor(rz_bias[:, :], bias_rows[:, 0, 0:2 * D], bias_rows[:, 1, 0:2 * D], ALU.add)\
              .then_inc(biases_ready, 1)
            for b in range(B):
                nc.vector.tensor_scalar(neg_b_hn[:, :, b], b_hn[:, :], -1.0, None, ALU.mult).then_inc(biases_ready, 1)
            dve.wait_ge(cleared, CLEARS)
            nc.vector.memset(third(cand_mul[:, :], 2), -1.0).then_inc(masks_ready, 1)
            nc.vector.memset(third(upd_mul[:, :], 1), 1.0).then_inc(masks_ready, 1)
            nc.vector.tensor_copy(hid_cols(0), cond[:, :, :]).then_inc(h_ready, 1)
            dve.wait_ge(biases_ready, BIASES)
            dve.wait_ge(masks_ready, 2)
            dve.wait_ge(pool_const, POOL_CONSTS)

            def turn_r(n):
                dve.wait_ge(r_summed, n + 1)
                nc.vector.transpose(turned_r[:, :], ps_r[:, 0:HALVES * QF]).then_inc(r_turned, 1)

            def turn_hn(n, s):
                dve.wait_ge(hn_summed, n + 1)
                nc.vector.transpose(turned_hn[:, :], ps_hn[:, 0:HALVES * QF]).then_inc(hn_turned, 1)
                dve.wait_ge(hn_turned, n + 1)
                nc.vector.tensor_tensor(third(cand_in[:, s, :], 0), neg_b_hn[:, :, :], turned(turned_hn), ALU.subtract)\
                  .then_inc(hn_placed, 1)

            def candidate(c, n, s):
                if s == 0:
                    dve.wait_ge(in_ready, HALVES * (c + 1))
                dve.wait_ge(r_ready, n + 1)
                dve.wait_ge(hn_placed, n + 1)
                nc.vector.tensor_tensor_scan(cand_out[:, :], cand_mul[:, :], cand_in[:, s, :], 0.0, ALU.mult, ALU.add)\
                  .then_inc(arg_ready, 1)

            def turn_z(n):
                dve.wait_ge(z_summed, n + 1)
                nc.vector.transpose(turned_z[:, :], ps_z[:, 0:HALVES * QF]).then_inc(z_turned, 1)

            def update(n, s):
                if runs_after(n, 2):
                    dve.wait_ge(hist_kept, n - 1)
                dve.wait_ge(n_ready, n + 1)
                dve.wait_ge(z_ready, n + 1)
                nc.vector.tensor_tensor_scan(hid[(s + 1) % 2][:, 0:3 * HB], upd_mul[:, :],
                                             hid[s % 2][:, 2:2 + 3 * HB], 0.0, ALU.mult, ALU.add).then_inc(h_ready, 1)

            def compare(values, which, op):
                at_j = values[:, None, :].to_broadcast([P, E0, E0])
                at_e = values[:, :, None].to_broadcast([P, E0, E0])
                return nc.vector.tensor_tensor(pairs[:, :, which, :], at_j, at_e, op)

            def unit_hidden(q, u):
                n = UNITS * q + u
                dve.wait_ge(sig_gate_ready, n + 1)
                if u == 0:
                    nc.vector.tensor_tensor(act_gate[:, :], ps_gu[:, 0:I0], sig_gate[:, :], ALU.mult)\
                      .then_inc(act_gate_ready, 1)
                else:
                    nc.vector.scalar_tensor_tensor(act_gate[:, :], ps_gu[:, 0:I0], probs[:, u - 1:u], sig_gate[:, :],
                                                   ALU.mult, ALU.mult).then_inc(act_gate_ready, 1)
                dve.wait_ge(act_gate_ready, n + 1)
                if runs_after(n, 1):
                    dve.wait_ge(hidden0_turned, n)
                if u == 0:
                    nc.vector.tensor_tensor(hidden0[:, :], ps_gu[:, I0:2 * I0], act_gate[:, :], ALU.mult)\
                      .then_inc(hidden0_ready, 1)
                else:
                    nc.vector.scalar_tensor_tensor(hidden0[:, :], ps_gu[:, I0:2 * I0], probs[:, u - 1:u],
                                                   act_gate[:, :], ALU.mult, ALU.mult).then_inc(hidden0_ready, 1)

            def moe0_part(q, s):
                if s == 2:
                    dve.wait_ge(logits0_summed, q + 1)
                    nc.vector.tensor_copy(logits0[:, :], ps_t[:, 0:E0]).then_inc(logits0_ready, 1)
                if s == 3:
                    dve.wait_ge(logits0_ready, q + 1)
                    compare(logits0, 0, ALU.is_gt)
                    compare(logits0, 1, ALU.is_equal).then_inc(rank0_step, 1)
                    dve.wait_ge(rank0_step, RANK_OPS * q + 1)
                    nc.vector.tensor_tensor(pairs[:, :, 1, :], pairs[:, :, 1, :], before[:, :, :], ALU.mult)\
                      .then_inc(rank0_step, 1)
                    dve.wait_ge(rank0_step, RANK_OPS * q + 2)
                    nc.vector.tensor_reduce(rank[:, :], pairs[:, :, :, :], AX.XY, ALU.add).then_inc(rank0_step, 1)
                    dve.wait_ge(rank0_step, RANK_OPS * q + 3)
                    dve.wait_ge(sig0_ready, q + 1)
                    nc.vector.scalar_tensor_tensor(probs[:, :], rank[:, :], 1.5, sig0[:, :], ALU.is_lt, ALU.mult)\
                      .then_inc(rank0_step, 1)
                u = unit_of(s, 2)
                if u is not None:
                    unit_hidden(q, u)
                if s == 30:
                    dve.wait_ge(down_summed, UNITS * (q + 1))
                    dve.wait_ge(x_res_loaded, 16 * (q + 1))
                    if runs_after(q, 1):
                        dve.wait_ge(carried, q)
                    nc.vector.tensor_tensor(x1[:, :, CARRY:CARRY + P],
                                            ps_moe0[:, 0:D].rearrange("p (c t) -> p c t", c=HALVES), x_res[:, :, :],
                                            ALU.add).then_inc(x1_ready, 1)

            def conv(q, tap):
                for half in range(HALVES):
                    src = x1[:, half, B * tap:B * tap + P]
                    w = cond[:, half, tap:tap + 1]
                    if tap == 0:
                        if runs_after(q, 1):
                            dve.wait_ge(proj1_summed, q)
                        nc.vector.tensor_scalar(y[:, half, :], src, w, conv_b[:, half:half + 1], ALU.mult, ALU.add)\
                          .then_inc(conv_step, 1)
                    else:
                        dve.wait_ge(conv_step, CONV_OPS * q + HALVES * (tap - 1) + half + 1)
                        nc.vector.scalar_tensor_tensor(y[:, half, :], src, w, y[:, half, :], ALU.mult, ALU.add)\
                          .then_inc(conv_step, 1)

            def soft(ins, q, k):
                ins.then_inc(soft_step, 1)
                dve.wait_ge(soft_step, SOFT_OPS * q + k)

            def moe1_part(q, s):
                if s == 0:
                    dve.wait_ge(x1_ready, q + 1)
                if s in (0, 1, 3, 4):
                    conv(q, (0, 1, 3, 4).index(s))
                if s == 10:
                    dve.wait_ge(proj1_summed, q + 1)
                    nc.vector.tensor_copy(hx1[:, :], ps_moe1[:, 0:E1 * I1 + E1]).then_inc(hx1_ready, 1)
                    dve.wait_ge(hx1_ready, q + 1)
                    nc.vector.tensor_reduce(top1[:, :], hx1[:, E1 * I1:E1 * I1 + E1], AX.X, ALU.max)\
                      .then_inc(top1_ready, 1)
                    dve.wait_ge(top1_ready, 2 * q + 1)
                    nc.vector.tensor_scalar(neg_top1[:, :], top1[:, :], -1.0, None, ALU.mult).then_inc(top1_ready, 1)
                if s == 12:
                    dve.wait_ge(exp_ready, 2 * (q + 1))
                    soft(nc.vector.reciprocal(sig_dn[:, :], sig_dn[:, :]), q, 1)
                    soft(nc.vector.tensor_tensor(expd[:, :], sig_up[:, :], sig_dn[:, :], ALU.mult), q, 2)
                    soft(nc.vector.tensor_reduce(total[:, :], expd[:, :], AX.X, ALU.add), q, 3)
                    soft(nc.vector.reciprocal(total[:, :], total[:, :]), q, 4)
                if s == 13:
                    soft(nc.vector.tensor_scalar(weights[:, :], expd[:, :], total[:, 0:1], None, ALU.mult), q, 5)
                    compare(weights, 0, ALU.is_gt)
                    soft(compare(weights, 1, ALU.is_equal), q, 6)
                    soft(nc.vector.tensor_tensor(pairs[:, :, 1, :], pairs[:, :, 1, :], before[:, :, :], ALU.mult), q, 7)
                if s == 15:
                    soft(nc.vector.tensor_reduce(rank[:, :], pairs[:, :, :, :], AX.XY, ALU.add), q, 8)
                    soft(nc.vector.scalar_tensor_tensor(gate1[:, :], rank[:, :], 1.5, weights[:, :], ALU.is_lt,
                                                        ALU.mult), q, 9)
                    dve.wait_ge(sig_hx_ready, q + 1)
                    nc.vector.tensor_tensor(act1[:, :], hx1[:, 0:E1 * I1], sig_hx[:, :], ALU.mult)\
                      .then_inc(act1_ready, 1)
                    dve.wait_ge(act1_ready, q + 1)
                    nc.vector.tensor_tensor(gated1[:, :].rearrange("p (e i) -> p e i", e=E1),
                                            act1[:, :].rearrange("p (e i) -> p e i", e=E1),
                                            gate1[:, :, None].to_broadcast([P, E1, I1]), ALU.mult)\
                      .then_inc(gated1_ready, 1)
                if s == 19:
                    dve.wait_ge(moe1_summed, q + 1)
                    if runs_after(q, 1):
                        dve.wait_ge(stored, 16 * q)
                    nc.vector.tensor_tensor(out_sb[:, :, :], ps_moe1[:, 0:D].rearrange("p (c t) -> p c t", c=HALVES),
                                            x1[:, :, CARRY:CARRY + P], ALU.add).then_inc(out_ready, 1)
                if s == 21:
                    nc.vector.tensor_copy(x1[:, :, 0:CARRY], x1[:, :, P:P + CARRY]).then_inc(carried, 1)

            def run(c, gru, pre, moe0, moe1):
                for s in range(STEPS):
                    if gru:
                        n = STEPS * c + s
                        turn_r(n)
                        turn_hn(n, s)
                        candidate(c, n, s)
                        turn_z(n)
                        update(n, s)
                    if moe1:
                        moe1_part(c - 2, s)
                    if moe0:
                        moe0_part(c - 1, s)

            iterations(dve, run)

        @block.tensor
        def _(pe):
            def input_rz(q, s, ps, gate):
                for quad in range(QUADS):
                    last = nc.tensor.matmul(gate_out(ps, quad), ident[:, B * s:B * s + B],
                                            gate_cols(gi_rz, None, gate, quad), start=True, stop=False,
                                            skip_group_check=True)
                return last

            def input_parts(q, s):
                n = STEPS * q + s
                if s == 0:
                    pe.wait_ge(gi_ready, q + 1)
                if runs_after(n, 1):
                    pe.wait_ge(r_turned, n)
                input_rz(q, s, ps_r, 0)
                if runs_after(n, 1):
                    pe.wait_ge(z_turned, n)
                last = input_rz(q, s, ps_z, 1)
                if s == STEPS - 1:
                    last.then_inc(gi_used, 1)

            def hidden_part(i, ps, gate, fresh):
                for k in range(HALVES):
                    for quad in range(QUADS):
                        last = nc.tensor.matmul(gate_out(ps, quad), hid_cols(i, k), gate_cols(w_hh, k, gate, quad),
                                                start=(fresh and k == 0), stop=(k == HALVES - 1), skip_group_check=True)
                return last

            def gru_step(c, s):
                n = STEPS * c + s
                pe.wait_ge(h_ready, n + 1)
                hidden_part(s, ps_r, 0, False).then_inc(r_summed, 1)
                hidden_part(s, ps_hn, 2, True).then_inc(hn_summed, 1)
                hidden_part(s, ps_z, 1, False).then_inc(z_summed, 1)

            COLS = 4
            PRE_PARTS = COLS + HALVES * COLS

            def pre_rz(q, j):
                if j == 0:
                    if runs_after(q, 1):
                        pe.wait_ge(gi_ready, q)
                k, col = j // COLS - 1, j % COLS
                dst = ps_gi[:, P * col:P * (col + 1)]
                if k < 0:
                    nc.tensor.matmul(dst, ones[0:1, 0, :], rz_bias[0:1, P * col:P * (col + 1)], start=(col == 0),
                                     stop=False, skip_group_check=True)
                    return
                if j == COLS:
                    pe.wait_ge(x_pre_loaded, 16 * (q + 1))
                last = nc.tensor.matmul(dst, x_pre[:, k, :], w_ih[:, k, P * col:P * (col + 1)], start=False,
                                        stop=(k == HALVES - 1), skip_group_check=True)
                if j == PRE_PARTS - 1:
                    last.then_inc(gi_summed, 1)

            def pre_in(q, j, moe1_done):
                half, k = j // HALVES, j % HALVES
                if j == 0:
                    if runs_after(q, 1):
                        pe.wait_ge(in_ready, HALVES * q)
                    if moe1_done is not None:
                        pe.wait_ge(out_ready, moe1_done)
                last = nc.tensor.matmul(ps_moe1[:, half * P:(half + 1) * P],
                                        w_ih[:, k, 2 * D + half * P:2 * D + (half + 1) * P], x_pre[:, k, :],
                                        start=(j == 0), stop=(k == HALVES - 1), skip_group_check=True)
                if j == 2 * HALVES - 1:
                    last.then_inc(in_summed, 1)

            def moe0_part(q, s):
                u = unit_of(s, 0)
                if u is not None:
                    n = UNITS * q + u
                    if u == 0:
                        pe.wait_ge(moe0_x_ready, q + 1)
                    if runs_after(n, 1):
                        pe.wait_ge(hidden0_ready, n)
                    nc.tensor.matmul(ps_gu[:, 0:2 * I0], moe0_x[:, 0, :], gate_up[:, u, 0, :], start=True, stop=False)
                u = unit_of(s, 1)
                if u is not None:
                    last = nc.tensor.matmul(ps_gu[:, 0:2 * I0], moe0_x[:, 1, :], gate_up[:, u, 1, :], start=False,
                                            stop=True)
                    last.then_inc(gu_summed, 1)
                if s == 2:
                    if runs_after(q, 1):
                        pe.wait_ge(hidden0_c_ready, UNITS * q)
                    for k in range(HALVES):
                        last = nc.tensor.matmul(ps_t[:, 0:E0], moe0_x[:, k, :], router0[:, k, :], start=(k == 0),
                                                stop=(k == HALVES - 1))
                    last.then_inc(logits0_summed, 1)
                u = unit_of(s, 3)
                if u is not None:
                    n = UNITS * q + u
                    pe.wait_ge(hidden0_ready, n + 1)
                    if u == 0:
                        pe.wait_ge(logits0_ready, q + 1)
                    else:
                        pe.wait_ge(hidden0_c_ready, n)
                    nc.tensor.transpose(ps_t[:, 0:P], hidden0[:, :], ident[:, :]).then_inc(hidden0_turned, 1)
                u = unit_of(s, 5)
                if u is not None:
                    n = UNITS * q + u
                    pe.wait_ge(hidden0_c_ready, n + 1)
                    if u == 0 and runs_after(q, 1):
                        pe.wait_ge(x1_ready, q)
                    for half in range(HALVES):
                        last = nc.tensor.matmul(ps_moe0[:, half * P:(half + 1) * P],
                                                down[:, u, half * P:(half + 1) * P], hidden0_c[:, :],
                                                start=(u == 0 and half == 0), stop=(u == UNITS - 1),
                                                skip_group_check=True)
                    last.then_inc(down_summed, 1)

            def moe1_part(q, s):
                if s in (8, 10):
                    k = (8, 10).index(s)
                    if k == 0:
                        pe.wait_ge(conv_step, CONV_OPS * (q + 1))
                        placed = min(q + 3, CHUNKS) if isinstance(q, int) else q + 3
                        pe.wait_ge(in_ready, HALVES * placed)
                        if runs_after(q, 1):
                            pe.wait_ge(out_ready, q)
                    last = nc.tensor.matmul(ps_moe1[:, 0:E1 * I1 + E1], y[:, k, :], proj1[:, k, :], start=(k == 0),
                                            stop=(k == HALVES - 1))
                    if k == HALVES - 1:
                        last.then_inc(proj1_summed, 1)
                if s == 17:
                    pe.wait_ge(gated1_ready, q + 1)
                    pe.wait_ge(hx1_ready, q + 1)
                    nc.tensor.transpose(ps_moe1[:, D:D + P], gated1[:, :], ident[:, :]).then_inc(gated1_turned, 1)
                if s == 19:
                    pe.wait_ge(gated1_c_ready, q + 1)
                    for half in range(HALVES):
                        last = nc.tensor.matmul(ps_moe1[:, half * P:(half + 1) * P], up1[:, half * P:(half + 1) * P],
                                                gated1_c[:, :], start=(half == 0), stop=True, skip_group_check=True)
                    last.then_inc(moe1_summed, 1)

            RZ_AT = (1, 4, 5, 7, 11, 13, 14, 16, 20, 22, 23, 25)
            IN_AT = (26, 28, 28, 30)

            def pre_part(q, s, moe1_done):
                for j, at in enumerate(RZ_AT):
                    if at == s:
                        pre_rz(q, j)
                for j, at in enumerate(IN_AT):
                    if at == s:
                        pre_in(q, j, moe1_done)

            def run(c, gru, pre, moe0, moe1):
                for s in range(STEPS):
                    if gru:
                        gru_step(c, s)
                    if moe0:
                        moe0_part(c - 1, s)
                    if moe1:
                        moe1_part(c - 2, s)
                    if pre:
                        pre_part(c + 1, s, c - 1 if moe1 else None)
                    if gru and s < STEPS - 1:
                        input_parts(c, s + 1)
                    elif pre:
                        input_parts(c + 1, 0)

            pe.wait_ge(pool_const, POOL_CONSTS)
            pe.wait_ge(biases_ready, BIASES)
            pe.wait_ge(cleared, CLEARS)
            pe.wait_ge(loaded_in, 16)
            for j in range(PRE_PARTS):
                pre_rz(0, j)
            for j in range(2 * HALVES):
                pre_in(0, j, None)
            input_parts(0, 0)
            pe.wait_ge(loaded_gru, 16)
            pe.wait_ge(loaded_moe, 16 * MOE_LOADS)
            iterations(pe, run)


def kernel(x, cond_2048, L0_cond_W_ih, L0_cond_W_hh, L0_cond_b_ih, L0_cond_b_hh, L0_ffn_router_w, L0_ffn_gate_up_w,
           L0_ffn_down_w, L0_ffn_shared_gate_w, L0_ffn_shared_up_w, L0_ffn_shared_down_w, L1_cond_b, L1_ffn_router_w,
           L1_ffn_down_w, L1_ffn_up_w):
    import numpy as np
    import concourse.bacc as bacc
    from concourse.bass_utils import run_bass_kernel_spmd

    def halves(w):
        w = np.asarray(w)
        return w.reshape((HALVES, P) + w.shape[1:]).swapaxes(0, 1)

    chunked = np.asarray(x).reshape(B, CHUNKS, STEPS, HALVES, P).transpose(1, 4, 3, 2, 0)
    arrays = {
        "x_c": chunked.reshape(CHUNKS, P, D),
        "h0_c": halves(np.asarray(cond_2048).T),
        "w_ih": halves(L0_cond_W_ih),
        "w_hh": halves(L0_cond_W_hh),
        "b_ih_row": np.asarray(L0_cond_b_ih).reshape(1, G3),
        "b_hh_row": np.asarray(L0_cond_b_hh).reshape(1, G3),
        "b_ih_c": halves(np.asarray(L0_cond_b_ih)[2 * D:]),
        "b_hh_c": halves(np.asarray(L0_cond_b_hh)[2 * D:]),
        "r0": halves(L0_ffn_router_w),
        "gu": np.asarray(L0_ffn_gate_up_w).reshape(E0, HALVES, P, 2 * I0).transpose(2, 0, 1, 3),
        "dn": np.asarray(L0_ffn_down_w).transpose(1, 0, 2),
        "sg": halves(L0_ffn_shared_gate_w),
        "su": halves(L0_ffn_shared_up_w),
        "sd": np.asarray(L0_ffn_shared_down_w),
        "conv_b": halves(L1_cond_b),
        "r1": halves(np.asarray(L1_ffn_router_w).T),
        "d1": halves(np.asarray(L1_ffn_down_w).transpose(2, 0, 1).reshape(D, E1 * I1)),
        "u1": np.asarray(L1_ffn_up_w).transpose(0, 2, 1).reshape(E1 * I1, D),
    }
    arrays = {f"in_{name}": np.ascontiguousarray(a) for name, a in arrays.items()}
    nc = bacc.Bacc("TRN2", target_bir_lowering=False, num_devices=1)
    args = [nc.dram_tensor(name, a.shape, mybir.dt.from_np(a.dtype), kind="ExternalInput").ap()
            for name, a in arrays.items()]
    out = nc.dram_tensor("out_c", (CHUNKS, P, D), F32, kind="ExternalOutput").ap()
    build(nc, *args, out)
    got = run_bass_kernel_spmd(nc, [arrays], core_ids=[0]).results[0]["out_c"]
    return got.reshape(CHUNKS, P, HALVES, STEPS, B).transpose(4, 0, 3, 2, 1).reshape(B, T, D)
```

```python
from contextlib import ExitStack

import concourse.bass as bass
from concourse import mybir

F32 = mybir.dt.float32
ALU = mybir.AluOpType
ACT = mybir.ActivationFunctionType
AX = mybir.AxisListType

P = 128
B = 4
D = 256
T = 256
HALVES = D // P
STEPS = P // B
CHUNKS = T // STEPS
G3 = 3 * D
HB = HALVES * B
QUADS = 4
QF = P // QUADS
E0, I0 = 8, 128
E1, I1 = 8, 16
UNITS = E0 + 1
TAPS = 4
CARRY = (TAPS - 1) * B


def build(nc, x_c, small_d, bias_d, w_ih_d, w_hh_d, r0_d, gu_d, dn_d, sg_d, su_d, sd_d, r1_d, d1_d, u1_d, out_c):
    with ExitStack() as ctx:
        def sb(name, shape, dt=F32):
            return ctx.enter_context(nc.sbuf_tensor(name, shape, dt))

        def bank(name, shape):
            return ctx.enter_context(nc.psum_tensor(name, shape, F32))

        def sem(name):
            return ctx.enter_context(nc.semaphore(name))

        w_ih = sb("w_ih", [P, HALVES, G3])
        w_hh = sb("w_hh", [P, HALVES, G3])
        gate_up = sb("gate_up", [P, UNITS, HALVES, 2 * I0])
        down = sb("down", [P, UNITS, D])
        router0 = sb("router0", [P, HALVES, E0])
        proj1 = sb("proj1", [P, HALVES, E1 * I1 + E1])
        up1 = sb("up1", [P, D])
        ident = sb("ident", [P, P])
        ones = sb("ones", [P, HALVES, P])
        bias_rows = sb("bias_rows", [1, 2, G3])
        rz_bias = sb("rz_bias", [1, 2 * D])
        neg_b_in = sb("neg_b_in", [P, HALVES])
        neg_b_hn = sb("neg_b_hn", [P, HALVES, B])
        small = sb("small", [P, HALVES, B + 3])
        cond = small[:, :, 0:B]
        b_in, b_hn, conv_b = (small[:, :, B + i] for i in range(3))
        table_warm = sb("table_warm", [P, 1])
        before = sb("before", [P, E0, E0])

        hid = [sb(f"hid{i}", [P, 3 * HB + 2]) for i in range(2)]
        turned_rh = sb("turned_rh", [P, 2 * HALVES * QF])
        turned_z = sb("turned_z", [P, HALVES * QF])
        cand_mul = sb("cand_mul", [P, 3 * HB])
        cand_out = sb("cand_out", [P, 3 * HB])
        upd_mul = sb("upd_mul", [P, 3 * HB])
        cand_in = sb("cand_in", [P, STEPS, 3 * HB])
        gi_rz = sb("gi_rz", [P, 2 * D])
        hist = sb("hist", [P, HALVES, P])
        moe0_x = sb("moe0_x", [P, HALVES, P])

        x_pre = sb("x_pre", [P, HALVES, P])
        x_res = sb("x_res", [P, HALVES, P])
        x1 = sb("x1", [P, HALVES, CARRY + P])
        logits0 = sb("logits0", [P, E0])
        sig0 = sb("sig0", [P, E0])
        pairs = sb("pairs", [P, E0, 2, E0])
        rank = sb("rank", [P, E0])
        probs = sb("probs", [P, E0])
        sig_gate = sb("sig_gate", [P, I0])
        act_gate = sb("act_gate", [P, I0])
        hidden0 = sb("hidden0", [P, I0])
        hidden0_c = sb("hidden0_c", [P, P])
        y = sb("y", [P, HALVES, P])
        hx1 = sb("hx1", [P, E1 * I1 + E1])
        top1 = sb("top1", [P, 1])
        neg_top1 = sb("neg_top1", [P, 1])
        sig_up = sb("sig_up", [P, E1])
        sig_dn = sb("sig_dn", [P, E1])
        expd = sb("expd", [P, E1])
        total = sb("total", [P, 1])
        weights = sb("weights", [P, E1])
        gate1 = sb("gate1", [P, E1])
        sig_hx = sb("sig_hx", [P, E1 * I1])
        act1 = sb("act1", [P, E1 * I1])
        gated1 = sb("gated1", [P, E1 * I1])
        gated1_c = sb("gated1_c", [P, P])
        out_sb = sb("out_sb", [P, HALVES, P])

        ps_rh = bank("ps_rh", [P, 512])
        ps_z = bank("ps_z", [P, 512])
        ps_gi = bank("ps_gi", [P, 512])
        ps_gu = bank("ps_gu", [P, 512])
        ps_gu2 = bank("ps_gu2", [P, 512])
        ps_t = bank("ps_t", [P, 512])
        ps_moe0 = bank("ps_moe0", [P, 512])
        ps_moe1 = bank("ps_moe1", [P, 512])

        loaded_gru = sem("loaded_gru")
        loaded_in = sem("loaded_in")
        loaded_small = sem("loaded_small")
        loaded_moe = sem("loaded_moe")
        pool_const = sem("pool_const")
        cleared = sem("cleared")
        biases_ready = sem("biases_ready")
        masks_ready = sem("masks_ready")
        x_pre_loaded = sem("x_pre_loaded")
        x_res_loaded = sem("x_res_loaded")
        stored = sem("stored")
        h_ready = sem("h_ready")
        rh_summed = sem("rh_summed")
        z_summed = sem("z_summed")
        rh_turned = sem("rh_turned")
        z_turned = sem("z_turned")
        cand_parts = sem("cand_parts")
        arg_ready = sem("arg_ready")
        n_ready = sem("n_ready")
        hist_kept = sem("hist_kept")
        gi_used = sem("gi_used")
        gi_summed = sem("gi_summed")
        gi_ready = sem("gi_ready")
        in_summed = sem("in_summed")
        in_ready = sem("in_ready")
        moe0_x_ready = sem("moe0_x_ready")
        logits0_summed = sem("logits0_summed")
        logits0_ready = sem("logits0_ready")
        sig0_ready = sem("sig0_ready")
        rank0_step = sem("rank0_step")
        gu_summed = sem("gu_summed")
        sig_gate_ready = sem("sig_gate_ready")
        act_gate_ready = sem("act_gate_ready")
        hidden0_ready = sem("hidden0_ready")
        hidden0_turned = sem("hidden0_turned")
        hidden0_c_ready = sem("hidden0_c_ready")
        down_summed = sem("down_summed")
        x1_ready = sem("x1_ready")
        conv_step = sem("conv_step")
        proj1_summed = sem("proj1_summed")
        hx1_ready = sem("hx1_ready")
        top1_ready = sem("top1_ready")
        exp_ready = sem("exp_ready")
        soft_step = sem("soft_step")
        sig_hx_ready = sem("sig_hx_ready")
        act1_ready = sem("act1_ready")
        gated1_ready = sem("gated1_ready")
        gated1_turned = sem("gated1_turned")
        gated1_c_ready = sem("gated1_c_ready")
        moe1_summed = sem("moe1_summed")
        out_ready = sem("out_ready")
        carried = sem("carried")

        WARM_UPS = 6
        SMALL_LOADS, MOE_LOADS = 2, 9
        CLEARS, BIASES, POOL_CONSTS = 8, 2 + B, 5
        CONV_OPS = HALVES * TAPS
        RANK_OPS = 4
        SOFT_OPS = 9

        def gate_cols(w, k, gate, quad):
            cols = w[:, k, gate * D:(gate + 1) * D] if k is not None else w[:, gate * D:(gate + 1) * D]
            return cols.rearrange("p (c q f) -> p c q f", c=HALVES, q=QUADS)[:, :, quad, :]

        def rh_cols(k, quad):
            return w_hh[:, k, :].rearrange("p (g c q f) -> p g c q f", c=HALVES, q=QUADS, f=QF)[:, 0:3:2, :, quad, :]

        def gate_out(ps, quad):
            return ps[QF * quad:QF * quad + B, 0:HALVES * QF].rearrange("p (c f) -> p c f", c=HALVES)

        def hid_cols(i, k=None):
            trip = hid[i % 2][:, 2:2 + 3 * HB].rearrange("p (c b three) -> p c b three", c=HALVES, b=B)
            return trip[:, :, :, 0] if k is None else trip[:, k, :, 0]

        def third(buf, i):
            return buf.rearrange("p (c b three) -> p c b three", c=HALVES, b=B)[:, :, :, i]

        def turned(buf, gate=0):
            cols = buf[:, gate * HALVES * QF:(gate + 1) * HALVES * QF]
            return cols.rearrange("p (c f) -> p c f", c=HALVES)[:, :, 0:B]

        def runs_after(n, least):
            return not isinstance(n, int) or n >= least

        FIRST_LOOP, LAST_LOOP = 2, CHUNKS - 2

        def iterations(eng, run):
            run(0, gru=True, pre=True, moe0=False, moe1=False)
            run(1, gru=True, pre=True, moe0=True, moe1=False)
            with eng.Fori(FIRST_LOOP, LAST_LOOP + 1) as c:
                run(c, gru=True, pre=True, moe0=True, moe1=True)
            run(CHUNKS - 1, gru=True, pre=False, moe0=True, moe1=True)
            run(CHUNKS, gru=False, pre=False, moe0=True, moe1=True)
            run(CHUNKS + 1, gru=False, pre=False, moe0=False, moe1=True)

        TAIL_STEPS = STEPS + 1

        def turn_at(gru):
            return 3 if gru else 4

        def down_at(gru):
            return 5 if gru else 8

        def gu_bank(u, gru):
            return ps_gu if gru or u % 2 == 0 else ps_gu2

        def unit_of(s, at):
            u, rest = divmod(s - at, 3)
            return u if rest == 0 and 0 <= u < UNITS else None

        block = ctx.enter_context(nc.Block())

        @block.sync
        def _(sp):
            sp.dma_start(small[:, :, :], small_d).then_inc(loaded_small, 16)
            sp.dma_start(bias_rows[:, :, :], bias_d).then_inc(loaded_small, 16)
            sp.dma_start(x_pre[:, :, :], x_c[0].rearrange("p (c t) -> p c t", c=HALVES)).then_inc(x_pre_loaded, 16)
            sp.dma_start(w_ih[:, :, :], w_ih_d).then_inc(loaded_in, 16)
            sp.dma_start(w_hh[:, :, :], w_hh_d).then_inc(loaded_gru, 16)
            sp.dma_start(gate_up[:, 1:UNITS, :, :], gu_d).then_inc(loaded_moe, 16)
            sp.dma_start(down[:, 1:UNITS, :], dn_d).then_inc(loaded_moe, 16)

            def run(c, gru, pre, moe0, moe1):
                if pre:
                    sp.wait_ge(in_summed, c + 1)
                    sp.dma_start(x_pre[:, :, :], x_c[c + 1].rearrange("p (c t) -> p c t", c=HALVES))\
                      .then_inc(x_pre_loaded, 16)
                if moe0:
                    if runs_after(c, 2):
                        sp.wait_ge(x1_ready, c - 1)
                    sp.dma_start(x_res[:, :, :], x_c[c - 1].rearrange("p (c t) -> p c t", c=HALVES))\
                      .then_inc(x_res_loaded, 16)
                if moe1:
                    sp.wait_ge(out_ready, c - 1)
                    sp.dma_start(out_c[c - 2].rearrange("p (c t) -> p c t", c=HALVES), out_sb[:, :, :])\
                      .then_inc(stored, 16)

            iterations(sp, run)
            sp.wait_ge(stored, 16 * CHUNKS)

        @block.gpsimd
        def _(pool):
            nc.gpsimd.memset(ident[:, :], 0.0).then_inc(pool_const, 1)
            nc.gpsimd.memset(before[:, :, :], 1.0).then_inc(pool_const, 1)
            nc.gpsimd.memset(ones[:, :, :], 1.0).then_inc(pool_const, 1)
            pool.wait_ge(pool_const, 3)
            nc.gpsimd.affine_select(out=ident[:, :], in_=ident[:, :], compare_op=ALU.not_equal, fill=1.0, base=0,
                                    pattern=[[-1, P]], channel_multiplier=1).then_inc(pool_const, 1)
            nc.gpsimd.affine_select(out=before[:, :, :], in_=before[:, :, :], compare_op=ALU.is_gt, fill=0.0, base=0,
                                    pattern=[[1, E0], [-1, E0]], channel_multiplier=0).then_inc(pool_const, 1)

            def run(c, gru, pre, moe0, moe1):
                if not gru:
                    return
                for s in range(STEPS):
                    pool.wait_ge(h_ready, STEPS * c + s + 2)
                    nc.gpsimd.tensor_tensor(hist[:, :, B * s:B * s + B], hid_cols(s + 1), ones[:, :, 0:B], ALU.mult)\
                      .then_inc(hist_kept, 1)
                if runs_after(c, 1):
                    pool.wait_ge(gu_summed, UNITS * c)
                pool.wait_ge(hist_kept, STEPS * (c + 1))
                nc.gpsimd.tensor_tensor(moe0_x[:, :, :], hist[:, :, :], ones[:, :, :], ALU.mult)\
                  .then_inc(moe0_x_ready, 1)
                pool.wait_ge(moe0_x_ready, c + 1)

            iterations(pool, run)

        @block.scalar
        def _(act):
            def copy_gi(q):
                act.wait_ge(gi_summed, q + 1)
                if runs_after(q, 1):
                    act.wait_ge(gi_used, q)
                nc.scalar.activation(gi_rz[:, :], ps_gi[:, :], ACT.Copy).then_inc(gi_ready, 1)

            def place_in(q):
                act.wait_ge(in_summed, q + 1)
                for half in range(HALVES):
                    dst = cand_in[:, :, :].rearrange("p s (c b three) -> p s c b three", c=HALVES, b=B)
                    nc.scalar.activation(
                        dst[:, :, half, :, 1],
                        ps_moe1[:, half * P:(half + 1) * P].rearrange("p (s b) -> p s b", b=B),
                        ACT.Identity, bias=neg_b_in[:, half:half + 1], scale=-1.0).then_inc(in_ready, 1)

            act.wait_ge(biases_ready, BIASES)
            act.wait_ge(cleared, CLEARS)
            nc.scalar.activation(table_warm[:, :], neg_b_in[:, 0:1], ACT.Sigmoid)
            copy_gi(0)
            place_in(0)
            act.dma_start(router0[:, :, :], r0_d).then_inc(loaded_moe, 16)
            act.dma_start(gate_up[:, 0, :, 0:I0], sg_d).then_inc(loaded_moe, 16)
            act.dma_start(gate_up[:, 0, :, I0:2 * I0], su_d).then_inc(loaded_moe, 16)
            act.dma_start(down[:, 0, :], sd_d).then_inc(loaded_moe, 16)
            act.dma_start(proj1[:, :, 0:E1 * I1], d1_d).then_inc(loaded_moe, 16)
            act.dma_start(proj1[:, :, E1 * I1:E1 * I1 + E1], r1_d).then_inc(loaded_moe, 16)
            act.dma_start(up1[:, :], u1_d).then_inc(loaded_moe, 16)

            def gru_step(c, s):
                n = STEPS * c + s
                act.wait_ge(rh_turned, n + 1)
                nc.scalar.activation(third(cand_mul[:, :], 1), turned(turned_rh), ACT.Sigmoid)\
                  .then_inc(cand_parts, 1)
                act.wait_ge(z_turned, n + 1)
                nc.scalar.activation(third(upd_mul[:, :], 2), turned(turned_z), ACT.Sigmoid)
                act.wait_ge(arg_ready, n + 1)
                trip_in = cand_out[:, :].rearrange("p (j three) -> p j three", three=3)[:, :, 1:3]
                trip_out = hid[s % 2][:, 2:2 + 3 * HB].rearrange("p (j three) -> p j three", three=3)[:, :, 1:3]
                nc.scalar.activation(trip_out, trip_in, ACT.Tanh).then_inc(n_ready, 1)

            def run(c, gru, pre, moe0, moe1):
                for s in range(STEPS if gru else TAIL_STEPS):
                    if gru:
                        gru_step(c, s)
                    if moe0:
                        q = c - 1
                        if s == 2:
                            act.wait_ge(logits0_ready, q + 1)
                            nc.scalar.activation(sig0[:, :], logits0[:, :], ACT.Sigmoid).then_inc(sig0_ready, 1)
                        u = unit_of(s, 1)
                        if u is not None:
                            n = UNITS * q + u
                            act.wait_ge(gu_summed, n + 1)
                            if u == 0:
                                if runs_after(q, 1):
                                    act.wait_ge(hidden0_ready, n)
                                nc.scalar.activation(sig_gate[:, :], gu_bank(u, gru)[:, 0:I0], ACT.Sigmoid)\
                                  .then_inc(sig_gate_ready, 1)
                            else:
                                act.wait_ge(hidden0_ready, n)
                                if u == 1:
                                    act.wait_ge(rank0_step, RANK_OPS * (q + 1))
                                nc.scalar.activation(sig_gate[:, :], gu_bank(u, gru)[:, 0:I0], ACT.Sigmoid,
                                                     scale=probs[:, u - 1:u]).then_inc(sig_gate_ready, 1)
                        u = unit_of(s, turn_at(gru))
                        if u is not None:
                            n = UNITS * q + u
                            act.wait_ge(hidden0_turned, n + 1)
                            if runs_after(n, 1):
                                act.wait_ge(down_summed, n)
                            nc.scalar.activation(hidden0_c[:, :], ps_t[:, 0:P], ACT.Copy).then_inc(hidden0_c_ready, 1)
                    if moe1:
                        q = c - 2
                        if s == 11:
                            act.wait_ge(top1_ready, 2 * (q + 1))
                            nc.scalar.activation(sig_up[:, :], hx1[:, E1 * I1:E1 * I1 + E1], ACT.Sigmoid,
                                                 bias=neg_top1[:, 0:1]).then_inc(exp_ready, 1)
                            nc.scalar.activation(sig_dn[:, :], hx1[:, E1 * I1:E1 * I1 + E1], ACT.Sigmoid,
                                                 bias=top1[:, 0:1], scale=-1.0).then_inc(exp_ready, 1)
                            nc.scalar.activation(sig_hx[:, :], hx1[:, 0:E1 * I1], ACT.Sigmoid).then_inc(sig_hx_ready, 1)
                        if s == 19:
                            act.wait_ge(gated1_turned, q + 1)
                            nc.scalar.activation(gated1_c[:, :], ps_moe1[:, D:D + P], ACT.Copy).then_inc(gated1_c_ready, 1)
                    if pre:
                        if s == STEPS - 2:
                            copy_gi(c + 1)
                        if s == STEPS - 1:
                            place_in(c + 1)

            iterations(act, run)

        @block.vector
        def _(dve):
            for part in (ps_rh[:, 0:2 * HALVES * QF], ps_z[:, 0:HALVES * QF], cand_mul[:, :], upd_mul[:, :],
                         cand_in[:, :, :], hid[0][:, :], hid[1][:, :], x1[:, :, 0:CARRY]):
                nc.vector.memset(part, 0.0).then_inc(cleared, 1)
            dve.wait_ge(loaded_small, 16 * SMALL_LOADS)
            nc.vector.tensor_scalar(neg_b_in[:, :], b_in[:, :], -1.0, None, ALU.mult).then_inc(biases_ready, 1)
            nc.vector.tensor_tensor(rz_bias[:, :], bias_rows[:, 0, 0:2 * D], bias_rows[:, 1, 0:2 * D], ALU.add)\
              .then_inc(biases_ready, 1)
            for b in range(B):
                nc.vector.tensor_scalar(neg_b_hn[:, :, b], b_hn[:, :], -1.0, None, ALU.mult).then_inc(biases_ready, 1)
            dve.wait_ge(cleared, CLEARS)
            nc.vector.memset(third(cand_mul[:, :], 2), -1.0).then_inc(masks_ready, 1)
            nc.vector.memset(third(upd_mul[:, :], 1), 1.0).then_inc(masks_ready, 1)
            nc.vector.tensor_copy(hid_cols(0), cond).then_inc(h_ready, 1)
            dve.wait_ge(biases_ready, BIASES)
            dve.wait_ge(masks_ready, 2)
            dve.wait_ge(pool_const, POOL_CONSTS)

            def turn_rh(n, s):
                dve.wait_ge(rh_summed, n + 1)
                nc.vector.transpose(turned_rh[:, :], ps_rh[:, 0:2 * HALVES * QF]).then_inc(rh_turned, 1)
                dve.wait_ge(rh_turned, n + 1)
                nc.vector.tensor_tensor(third(cand_in[:, s, :], 0), neg_b_hn[:, :, :], turned(turned_rh, 1),
                                        ALU.subtract).then_inc(cand_parts, 1)

            def candidate(c, n, s):
                dve.wait_ge(cand_parts, 2 * (n + 1))
                if s == 0:
                    dve.wait_ge(in_ready, HALVES * (c + 1))
                nc.vector.tensor_tensor_scan(cand_out[:, :], cand_mul[:, :], cand_in[:, s, :], 0.0, ALU.mult, ALU.add)\
                  .then_inc(arg_ready, 1)

            def turn_z(n):
                dve.wait_ge(z_summed, n + 1)
                nc.vector.transpose(turned_z[:, :], ps_z[:, 0:HALVES * QF]).then_inc(z_turned, 1)

            def update(n, s):
                dve.wait_ge(n_ready, n + 1)
                if runs_after(n, 2):
                    dve.wait_ge(hist_kept, n - 1)
                nc.vector.tensor_tensor_scan(hid[(s + 1) % 2][:, 0:3 * HB], upd_mul[:, :],
                                             hid[s % 2][:, 2:2 + 3 * HB], 0.0, ALU.mult, ALU.add).then_inc(h_ready, 1)

            def compare(values, which, op):
                at_j = values[:, None, :].to_broadcast([P, E0, E0])
                at_e = values[:, :, None].to_broadcast([P, E0, E0])
                return nc.vector.tensor_tensor(pairs[:, :, which, :], at_j, at_e, op)

            def unit_hidden(q, u, ps_gu):
                n = UNITS * q + u
                dve.wait_ge(sig_gate_ready, n + 1)
                if u == 0:
                    nc.vector.tensor_tensor(act_gate[:, :], ps_gu[:, 0:I0], sig_gate[:, :], ALU.mult)\
                      .then_inc(act_gate_ready, 1)
                else:
                    nc.vector.scalar_tensor_tensor(act_gate[:, :], ps_gu[:, 0:I0], probs[:, u - 1:u], sig_gate[:, :],
                                                   ALU.mult, ALU.mult).then_inc(act_gate_ready, 1)
                dve.wait_ge(act_gate_ready, n + 1)
                if runs_after(n, 1):
                    dve.wait_ge(hidden0_turned, n)
                if u == 0:
                    nc.vector.tensor_tensor(hidden0[:, :], ps_gu[:, I0:2 * I0], act_gate[:, :], ALU.mult)\
                      .then_inc(hidden0_ready, 1)
                else:
                    nc.vector.scalar_tensor_tensor(hidden0[:, :], ps_gu[:, I0:2 * I0], probs[:, u - 1:u],
                                                   act_gate[:, :], ALU.mult, ALU.mult).then_inc(hidden0_ready, 1)

            def moe0_part(q, s, gru):
                if s == 2:
                    dve.wait_ge(logits0_summed, q + 1)
                    nc.vector.tensor_copy(logits0[:, :], ps_t[:, 0:E0]).then_inc(logits0_ready, 1)
                if s == 3:
                    dve.wait_ge(logits0_ready, q + 1)
                    compare(logits0, 0, ALU.is_gt)
                    compare(logits0, 1, ALU.is_equal).then_inc(rank0_step, 1)
                    dve.wait_ge(rank0_step, RANK_OPS * q + 1)
                    nc.vector.tensor_tensor(pairs[:, :, 1, :], pairs[:, :, 1, :], before[:, :, :], ALU.mult)\
                      .then_inc(rank0_step, 1)
                if s == 4:
                    dve.wait_ge(rank0_step, RANK_OPS * q + 2)
                    nc.vector.tensor_reduce(rank[:, :], pairs[:, :, :, :], AX.XY, ALU.add).then_inc(rank0_step, 1)
                    dve.wait_ge(rank0_step, RANK_OPS * q + 3)
                    dve.wait_ge(sig0_ready, q + 1)
                    nc.vector.scalar_tensor_tensor(probs[:, :], rank[:, :], 1.5, sig0[:, :], ALU.is_lt, ALU.mult)\
                      .then_inc(rank0_step, 1)
                u = unit_of(s, 2)
                if u is not None:
                    unit_hidden(q, u, gu_bank(u, gru))
                if s == (STEPS - 2 if gru else TAIL_STEPS - 1):
                    dve.wait_ge(down_summed, UNITS * (q + 1))
                    dve.wait_ge(x_res_loaded, 16 * (q + 1))
                    if runs_after(q, 1):
                        dve.wait_ge(carried, q)
                    nc.vector.tensor_tensor(x1[:, :, CARRY:CARRY + P],
                                            ps_moe0[:, 0:D].rearrange("p (c t) -> p c t", c=HALVES), x_res[:, :, :],
                                            ALU.add).then_inc(x1_ready, 1)

            def conv(q, tap):
                for half in range(HALVES):
                    src = x1[:, half, B * tap:B * tap + P]
                    w = cond[:, half, tap:tap + 1]
                    if tap == 0:
                        if runs_after(q, 1):
                            dve.wait_ge(proj1_summed, q)
                        nc.vector.tensor_scalar(y[:, half, :], src, w, conv_b[:, half:half + 1], ALU.mult, ALU.add)\
                          .then_inc(conv_step, 1)
                    else:
                        dve.wait_ge(conv_step, CONV_OPS * q + HALVES * (tap - 1) + half + 1)
                        nc.vector.scalar_tensor_tensor(y[:, half, :], src, w, y[:, half, :], ALU.mult, ALU.add)\
                          .then_inc(conv_step, 1)

            def soft_before(q, k):
                dve.wait_ge(soft_step, SOFT_OPS * q + k - 1)

            def moe1_part(q, s):
                if s == 0:
                    dve.wait_ge(x1_ready, q + 1)
                if s in (0, 1, 6, 7):
                    conv(q, (0, 1, 6, 7).index(s))
                if s == 10:
                    dve.wait_ge(proj1_summed, q + 1)
                    nc.vector.tensor_copy(hx1[:, :], ps_moe1[:, 0:E1 * I1 + E1]).then_inc(hx1_ready, 1)
                    dve.wait_ge(hx1_ready, q + 1)
                    nc.vector.tensor_reduce(top1[:, :], hx1[:, E1 * I1:E1 * I1 + E1], AX.X, ALU.max)\
                      .then_inc(top1_ready, 1)
                    dve.wait_ge(top1_ready, 2 * q + 1)
                    nc.vector.tensor_scalar(neg_top1[:, :], top1[:, :], -1.0, None, ALU.mult).then_inc(top1_ready, 1)
                if s == 12:
                    dve.wait_ge(exp_ready, 2 * (q + 1))
                    nc.vector.reciprocal(sig_dn[:, :], sig_dn[:, :]).then_inc(soft_step, 1)
                    soft_before(q, 2)
                    nc.vector.tensor_tensor(expd[:, :], sig_up[:, :], sig_dn[:, :], ALU.mult).then_inc(soft_step, 1)
                    soft_before(q, 3)
                    nc.vector.tensor_reduce(total[:, :], expd[:, :], AX.X, ALU.add).then_inc(soft_step, 1)
                if s == 13:
                    soft_before(q, 4)
                    nc.vector.reciprocal(total[:, :], total[:, :]).then_inc(soft_step, 1)
                    soft_before(q, 5)
                    nc.vector.tensor_scalar(weights[:, :], expd[:, :], total[:, 0:1], None, ALU.mult)\
                      .then_inc(soft_step, 1)
                if s == 15:
                    soft_before(q, 6)
                    compare(weights, 0, ALU.is_gt)
                    compare(weights, 1, ALU.is_equal).then_inc(soft_step, 1)
                    soft_before(q, 7)
                    nc.vector.tensor_tensor(pairs[:, :, 1, :], pairs[:, :, 1, :], before[:, :, :], ALU.mult)\
                      .then_inc(soft_step, 1)
                if s == 16:
                    soft_before(q, 8)
                    nc.vector.tensor_reduce(rank[:, :], pairs[:, :, :, :], AX.XY, ALU.add).then_inc(soft_step, 1)
                    soft_before(q, 9)
                    nc.vector.scalar_tensor_tensor(gate1[:, :], rank[:, :], 1.5, weights[:, :], ALU.is_lt, ALU.mult)\
                      .then_inc(soft_step, 1)
                if s == 18:
                    dve.wait_ge(sig_hx_ready, q + 1)
                    nc.vector.tensor_tensor(act1[:, :], hx1[:, 0:E1 * I1], sig_hx[:, :], ALU.mult)\
                      .then_inc(act1_ready, 1)
                    dve.wait_ge(act1_ready, q + 1)
                    dve.wait_ge(soft_step, SOFT_OPS * (q + 1))
                    nc.vector.tensor_tensor(gated1[:, :].rearrange("p (e i) -> p e i", e=E1),
                                            act1[:, :].rearrange("p (e i) -> p e i", e=E1),
                                            gate1[:, :, None].to_broadcast([P, E1, I1]), ALU.mult)\
                      .then_inc(gated1_ready, 1)
                if s == 24:
                    dve.wait_ge(moe1_summed, q + 1)
                    if runs_after(q, 1):
                        dve.wait_ge(stored, 16 * q)
                    nc.vector.tensor_tensor(out_sb[:, :, :], ps_moe1[:, 0:D].rearrange("p (c t) -> p c t", c=HALVES),
                                            x1[:, :, CARRY:CARRY + P], ALU.add).then_inc(out_ready, 1)
                if s == 25:
                    nc.vector.tensor_copy(x1[:, :, 0:CARRY], x1[:, :, P:P + CARRY]).then_inc(carried, 1)

            def run(c, gru, pre, moe0, moe1):
                for s in range(STEPS if gru else TAIL_STEPS):
                    if gru:
                        n = STEPS * c + s
                        turn_rh(n, s)
                        turn_z(n)
                        candidate(c, n, s)
                        update(n, s)
                    if moe0:
                        moe0_part(c - 1, s, gru)
                    if moe1:
                        moe1_part(c - 2, s)

            iterations(dve, run)

        @block.tensor
        def _(pe):
            def input_rz(q, s, ps, gate):
                for quad in range(QUADS):
                    last = nc.tensor.matmul(gate_out(ps, quad), ident[:, B * s:B * s + B],
                                            gate_cols(gi_rz, None, gate, quad), start=True, stop=False,
                                            skip_group_check=True)
                return last

            def input_parts(q, s):
                n = STEPS * q + s
                if s == 0:
                    pe.wait_ge(gi_ready, q + 1)
                if runs_after(n, 1):
                    pe.wait_ge(rh_turned, n)
                input_rz(q, s, ps_rh, 0)
                if runs_after(n, 1):
                    pe.wait_ge(z_turned, n)
                last = input_rz(q, s, ps_z, 1)
                if s == STEPS - 1:
                    last.then_inc(gi_used, 1)


            def gru_step(c, s):
                n = STEPS * c + s
                pe.wait_ge(h_ready, n + 1)
                for k in range(HALVES):
                    for quad in range(QUADS):
                        dst = ps_rh[QF * quad:QF * quad + B, 0:2 * HALVES * QF]
                        last = nc.tensor.matmul(dst.rearrange("p (g c f) -> p g c f", g=2, c=HALVES), hid_cols(s, k),
                                                rh_cols(k, quad), start=False, stop=(k == HALVES - 1),
                                                skip_group_check=True)
                last.then_inc(rh_summed, 1)
                for k in range(HALVES):
                    for quad in range(QUADS):
                        last = nc.tensor.matmul(gate_out(ps_z, quad), hid_cols(s, k), gate_cols(w_hh, k, 1, quad),
                                                start=False, stop=(k == HALVES - 1), skip_group_check=True)
                last.then_inc(z_summed, 1)

            COLS = 4
            PRE_PARTS = COLS + HALVES * COLS

            def pre_rz(q, j):
                if j == 0:
                    if runs_after(q, 1):
                        pe.wait_ge(gi_ready, q)
                k, col = j // COLS - 1, j % COLS
                dst = ps_gi[:, P * col:P * (col + 1)]
                if k < 0:
                    nc.tensor.matmul(dst, ones[0:1, 0, :], rz_bias[0:1, P * col:P * (col + 1)], start=(col == 0),
                                     stop=False, skip_group_check=True)
                    return
                if j == COLS:
                    pe.wait_ge(x_pre_loaded, 16 * (q + 1))
                last = nc.tensor.matmul(dst, x_pre[:, k, :], w_ih[:, k, P * col:P * (col + 1)], start=False,
                                        stop=(k == HALVES - 1), skip_group_check=True)
                if j == PRE_PARTS - 1:
                    last.then_inc(gi_summed, 1)

            def pre_in(q, j, moe1_done):
                half, k = j // HALVES, j % HALVES
                if j == 0:
                    if runs_after(q, 1):
                        pe.wait_ge(in_ready, HALVES * q)
                    if moe1_done is not None:
                        pe.wait_ge(out_ready, moe1_done)
                last = nc.tensor.matmul(ps_moe1[:, half * P:(half + 1) * P],
                                        w_ih[:, k, 2 * D + half * P:2 * D + (half + 1) * P], x_pre[:, k, :],
                                        start=(j == 0), stop=(k == HALVES - 1), skip_group_check=True)
                if j == 2 * HALVES - 1:
                    last.then_inc(in_summed, 1)

            def moe0_part(q, s, gru):
                u = unit_of(s, 0)
                if u is not None:
                    n = UNITS * q + u
                    if u == 0:
                        pe.wait_ge(moe0_x_ready, q + 1)
                    if gru and runs_after(n, 1):
                        pe.wait_ge(hidden0_ready, n)
                    elif not gru:
                        pe.wait_ge(hidden0_ready, n - 1)
                    nc.tensor.matmul(gu_bank(u, gru)[:, 0:2 * I0], moe0_x[:, 0, :], gate_up[:, u, 0, :], start=True, stop=False)
                u = unit_of(s, 1)
                if u is not None:
                    last = nc.tensor.matmul(gu_bank(u, gru)[:, 0:2 * I0], moe0_x[:, 1, :], gate_up[:, u, 1, :], start=False,
                                            stop=True)
                    last.then_inc(gu_summed, 1)
                if s == 2:
                    if runs_after(q, 1):
                        pe.wait_ge(hidden0_c_ready, UNITS * q)
                    for k in range(HALVES):
                        last = nc.tensor.matmul(ps_t[:, 0:E0], moe0_x[:, k, :], router0[:, k, :], start=(k == 0),
                                                stop=(k == HALVES - 1))
                    last.then_inc(logits0_summed, 1)
                u = unit_of(s, turn_at(gru))
                if u is not None:
                    n = UNITS * q + u
                    pe.wait_ge(hidden0_ready, n + 1)
                    if u == 0:
                        pe.wait_ge(logits0_ready, q + 1)
                    else:
                        pe.wait_ge(hidden0_c_ready, n)
                    nc.tensor.transpose(ps_t[:, 0:P], hidden0[:, :], ident[:, :]).then_inc(hidden0_turned, 1)
                u = unit_of(s, down_at(gru))
                if u is not None:
                    n = UNITS * q + u
                    pe.wait_ge(hidden0_c_ready, n + 1)
                    if u == 0 and runs_after(q, 1):
                        pe.wait_ge(x1_ready, q)
                    for half in range(HALVES):
                        last = nc.tensor.matmul(ps_moe0[:, half * P:(half + 1) * P],
                                                down[:, u, half * P:(half + 1) * P], hidden0_c[:, :],
                                                start=(u == 0 and half == 0), stop=(u == UNITS - 1),
                                                skip_group_check=True)
                    last.then_inc(down_summed, 1)

            def moe1_part(q, s):
                if s in (8, 10):
                    k = (8, 10).index(s)
                    if k == 0:
                        pe.wait_ge(conv_step, CONV_OPS * (q + 1))
                        placed = min(q + 3, CHUNKS) if isinstance(q, int) else q + 3
                        pe.wait_ge(in_ready, HALVES * placed)
                        if runs_after(q, 1):
                            pe.wait_ge(out_ready, q)
                    last = nc.tensor.matmul(ps_moe1[:, 0:E1 * I1 + E1], y[:, k, :], proj1[:, k, :], start=(k == 0),
                                            stop=(k == HALVES - 1))
                    if k == HALVES - 1:
                        last.then_inc(proj1_summed, 1)
                if s == 19:
                    pe.wait_ge(gated1_ready, q + 1)
                    pe.wait_ge(hx1_ready, q + 1)
                    nc.tensor.transpose(ps_moe1[:, D:D + P], gated1[:, :], ident[:, :]).then_inc(gated1_turned, 1)
                if s in (20, 22):
                    half = (20, 22).index(s)
                    if half == 0:
                        pe.wait_ge(gated1_c_ready, q + 1)
                    last = nc.tensor.matmul(ps_moe1[:, half * P:(half + 1) * P], up1[:, half * P:(half + 1) * P],
                                            gated1_c[:, :], start=(half == 0), stop=True, skip_group_check=True)
                    if half == HALVES - 1:
                        last.then_inc(moe1_summed, 1)

            RZ_AT = (1, 4, 5, 7, 11, 13, 14, 16, 17, 23, 25, 28)
            IN_AT = (26, 28, 28, 30)

            def pre_part(q, s, moe1_done):
                for j, at in enumerate(RZ_AT):
                    if at == s:
                        pre_rz(q, j)
                for j, at in enumerate(IN_AT):
                    if at == s:
                        pre_in(q, j, moe1_done)

            def keep_warm():
                nc.tensor.matmul(ps_gu2[:, 0:D], ident[:, :], ones[:, :, :], start=True, stop=True)

            def run(c, gru, pre, moe0, moe1):
                if isinstance(c, int) and c == 1:
                    pe.wait_ge(loaded_moe, 16 * MOE_LOADS)
                for s in range(STEPS if gru else TAIL_STEPS):
                    if gru:
                        gru_step(c, s)
                    if moe0:
                        moe0_part(c - 1, s, gru)
                    if moe1:
                        moe1_part(c - 2, s)
                    if pre:
                        pre_part(c + 1, s, c - 1 if moe1 else None)
                    if gru and not moe0:
                        keep_warm()
                    if gru and s < STEPS - 1:
                        input_parts(c, s + 1)
                    elif pre:
                        input_parts(c + 1, 0)

            pe.wait_ge(pool_const, POOL_CONSTS)
            for _ in range(WARM_UPS):
                keep_warm()
            pe.wait_ge(biases_ready, BIASES)
            pe.wait_ge(cleared, CLEARS)
            pe.wait_ge(loaded_in, 16)
            for j in range(PRE_PARTS):
                pre_rz(0, j)
            for j in range(2 * HALVES):
                pre_in(0, j, None)
            input_parts(0, 0)
            pe.wait_ge(loaded_gru, 16)
            iterations(pe, run)


def kernel(x, cond_2048, L0_cond_W_ih, L0_cond_W_hh, L0_cond_b_ih, L0_cond_b_hh, L0_ffn_router_w, L0_ffn_gate_up_w,
           L0_ffn_down_w, L0_ffn_shared_gate_w, L0_ffn_shared_up_w, L0_ffn_shared_down_w, L1_cond_b, L1_ffn_router_w,
           L1_ffn_down_w, L1_ffn_up_w):
    import numpy as np
    import concourse.bacc as bacc
    from concourse.bass_utils import run_bass_kernel_spmd

    def halves(w):
        w = np.asarray(w)
        return w.reshape((HALVES, P) + w.shape[1:]).swapaxes(0, 1)

    chunked = np.asarray(x).reshape(B, CHUNKS, STEPS, HALVES, P).transpose(1, 4, 3, 2, 0)
    arrays = {
        "x_c": chunked.reshape(CHUNKS, P, D),
        "small": np.concatenate([halves(np.asarray(cond_2048).T)] + [
            halves(np.asarray(v))[:, :, None] for v in (L0_cond_b_ih[2 * D:], L0_cond_b_hh[2 * D:], L1_cond_b)], axis=2),
        "bias": np.stack([np.asarray(L0_cond_b_ih), np.asarray(L0_cond_b_hh)])[None],
        "w_ih": halves(L0_cond_W_ih),
        "w_hh": halves(L0_cond_W_hh),
        "r0": halves(L0_ffn_router_w),
        "gu": np.asarray(L0_ffn_gate_up_w).reshape(E0, HALVES, P, 2 * I0).transpose(2, 0, 1, 3),
        "dn": np.asarray(L0_ffn_down_w).transpose(1, 0, 2),
        "sg": halves(L0_ffn_shared_gate_w),
        "su": halves(L0_ffn_shared_up_w),
        "sd": np.asarray(L0_ffn_shared_down_w),
        "r1": halves(np.asarray(L1_ffn_router_w).T),
        "d1": halves(np.asarray(L1_ffn_down_w).transpose(2, 0, 1).reshape(D, E1 * I1)),
        "u1": np.asarray(L1_ffn_up_w).transpose(0, 2, 1).reshape(E1 * I1, D),
    }
    arrays = {f"in_{name}": np.ascontiguousarray(a) for name, a in arrays.items()}
    nc = bacc.Bacc("TRN2", target_bir_lowering=False, num_devices=1)
    args = [nc.dram_tensor(name, a.shape, mybir.dt.from_np(a.dtype), kind="ExternalInput").ap()
            for name, a in arrays.items()]
    out = nc.dram_tensor("out_c", (CHUNKS, P, D), F32, kind="ExternalOutput").ap()
    build(nc, *args, out)
    got = run_bass_kernel_spmd(nc, [arrays], core_ids=[0]).results[0]["out_c"]
    return got.reshape(CHUNKS, P, HALVES, STEPS, B).transpose(4, 0, 3, 2, 1).reshape(B, T, D)
```

```python
from contextlib import ExitStack

import concourse.bass as bass
from concourse import mybir

F32 = mybir.dt.float32
ALU = mybir.AluOpType
ACT = mybir.ActivationFunctionType
AX = mybir.AxisListType

P = 128
B = 4
D = 256
T = 256
HALVES = D // P
STEPS = P // B
CHUNKS = T // STEPS
G3 = 3 * D
HB = HALVES * B
QUADS = 4
QF = P // QUADS
BLOCK = HALVES * QF
E0, I0 = 8, 128
E1, I1 = 8, 16
UNITS = E0 + 1
TAPS = 4
CARRY = (TAPS - 1) * B


def build(nc, x_c, small_d, bias_d, w_ih_d, w_hh_d, r0_d, gu_d, dn_d, sg_d, su_d, sd_d, r1_d, d1_d, u1_d, out_c):
    with ExitStack() as ctx:
        def sb(name, shape, dt=F32):
            return ctx.enter_context(nc.sbuf_tensor(name, shape, dt))

        def bank(name, shape):
            return ctx.enter_context(nc.psum_tensor(name, shape, F32))

        def sem(name):
            return ctx.enter_context(nc.semaphore(name))

        w_ih = sb("w_ih", [P, HALVES, G3])
        w_hh = sb("w_hh", [P, HALVES, G3])
        gate_up = sb("gate_up", [P, UNITS, HALVES, 2 * I0])
        down = sb("down", [P, UNITS, D])
        router0 = sb("router0", [P, HALVES, E0])
        proj1 = sb("proj1", [P, HALVES, E1 * I1 + E1])
        up1 = sb("up1", [P, D])
        ident = sb("ident", [P, P])
        ones = sb("ones", [P, HALVES, P])
        z_bias_rows = sb("z_bias_rows", [1, 2, D])
        z_bias = sb("z_bias", [1, D])
        r_bias = sb("r_bias", [P, HALVES])
        small = sb("small", [P, HALVES, B + 5])
        cond = small[:, :, 0:B]
        b_in, b_hn, conv_b, b_ir, b_hr = (small[:, :, B + i] for i in range(5))
        table_warm = sb("table_warm", [P, 1])
        before = sb("before", [P, E0, E0])

        hid = [sb(f"hid{i}", [P, 3 * HB + 2]) for i in range(2)]
        turned_r = sb("turned_r", [P, BLOCK])
        r_arg = sb("r_arg", [P, HALVES, B])
        z_rows = sb("z_rows", [P, BLOCK])
        cand_mul = sb("cand_mul", [P, 4 * HB])
        cand_in = sb("cand_in", [P, (STEPS - 1) * 4 * HB + 4 * BLOCK])
        cand_out = sb("cand_out", [P, 4 * HB])
        upd_mul = sb("upd_mul", [P, 3 * BLOCK])
        gi_z = sb("gi_z", [P, D])
        gi_r = sb("gi_r", [P, HALVES, STEPS, B])
        hist = sb("hist", [P, HALVES, P])
        moe0_x = sb("moe0_x", [P, HALVES, P])

        x_pre = sb("x_pre", [P, HALVES, P])
        x_res = sb("x_res", [P, HALVES, P])
        x1 = sb("x1", [P, HALVES, CARRY + P])
        logits0 = sb("logits0", [P, E0])
        sig0 = sb("sig0", [P, E0])
        pairs = sb("pairs", [P, E0, 2, E0])
        rank = sb("rank", [P, E0])
        probs = sb("probs", [P, E0])
        sig_gate = [sb(f"sig_gate{i}", [P, I0]) for i in range(2)]
        act_gate = [sb(f"act_gate{i}", [P, I0]) for i in range(2)]
        hidden0 = [sb(f"hidden0_{i}", [P, I0]) for i in range(2)]
        hidden0_c = [sb(f"hidden0_c_{i}", [P, P]) for i in range(2)]
        y = sb("y", [P, HALVES, P])
        logits1 = sb("logits1", [P, E1])
        top1 = sb("top1", [P, 1])
        neg_top1 = sb("neg_top1", [P, 1])
        sig_up = sb("sig_up", [P, E1])
        sig_dn = sb("sig_dn", [P, E1])
        expd = sb("expd", [P, E1])
        total = sb("total", [P, 1])
        chosen = sb("chosen", [P, E1])
        gate1 = sb("gate1", [P, E1])
        sig_hx = sb("sig_hx", [P, E1 * I1])
        act1 = sb("act1", [P, E1 * I1])
        gated1 = sb("gated1", [P, E1 * I1])
        gated1_c = sb("gated1_c", [P, P])
        out_sb = sb("out_sb", [P, HALVES, P])

        ps_r = bank("ps_r", [P, 512])
        ps_hn = bank("ps_hn", [P, 512])
        ps_z = bank("ps_z", [P, 512])
        ps_gi = bank("ps_gi", [P, 512])
        ps_gu = bank("ps_gu", [P, 512])
        ps_t = bank("ps_t", [P, 512])
        ps_moe0 = bank("ps_moe0", [P, 512])
        ps_moe1 = bank("ps_moe1", [P, 512])

        loaded_gru = sem("loaded_gru")
        loaded_in_rz = sem("loaded_in_rz")
        loaded_in_n = sem("loaded_in_n")
        loaded_small = sem("loaded_small")
        loaded_moe = sem("loaded_moe")
        pool_const = sem("pool_const")
        cleared = sem("cleared")
        biases_ready = sem("biases_ready")
        masks_ready = sem("masks_ready")
        x_pre_loaded = sem("x_pre_loaded")
        x_res_loaded = sem("x_res_loaded")
        stored = sem("stored")
        h_ready = sem("h_ready")
        r_summed = sem("r_summed")
        hn_summed = sem("hn_summed")
        z_summed = sem("z_summed")
        r_turned = sem("r_turned")
        r_arg_ready = sem("r_arg_ready")
        z_rows_ready = sem("z_rows_ready")
        cand_parts = sem("cand_parts")
        arg_ready = sem("arg_ready")
        upd_parts = sem("upd_parts")
        hist_kept = sem("hist_kept")
        gi_used = sem("gi_used")
        gi_summed = sem("gi_summed")
        gi_z_ready = sem("gi_z_ready")
        gi_r_ready = sem("gi_r_ready")
        in_summed = sem("in_summed")
        in_ready = sem("in_ready")
        moe0_x_ready = sem("moe0_x_ready")
        logits0_summed = sem("logits0_summed")
        logits0_ready = sem("logits0_ready")
        sig0_ready = sem("sig0_ready")
        rank0_step = sem("rank0_step")
        gu_summed = sem("gu_summed")
        sig_gate_ready = sem("sig_gate_ready")
        act_gate_ready = sem("act_gate_ready")
        hidden0_ready = sem("hidden0_ready")
        hidden0_turned = sem("hidden0_turned")
        hidden0_c_ready = sem("hidden0_c_ready")
        down_summed = sem("down_summed")
        x1_ready = sem("x1_ready")
        conv_step = sem("conv_step")
        proj1_summed = sem("proj1_summed")
        logits1_ready = sem("logits1_ready")
        top1_ready = sem("top1_ready")
        exp_ready = sem("exp_ready")
        rank1_step = sem("rank1_step")
        soft_step = sem("soft_step")
        sig_hx_ready = sem("sig_hx_ready")
        act1_ready = sem("act1_ready")
        gated1_ready = sem("gated1_ready")
        gated1_turned = sem("gated1_turned")
        gated1_c_ready = sem("gated1_c_ready")
        moe1_summed = sem("moe1_summed")
        out_ready = sem("out_ready")
        carried = sem("carried")

        WARM_UPS = 4
        SMALL_LOADS, MOE_LOADS = 2, 9
        CLEARS, BIASES, POOL_CONSTS = 10, 2 + HALVES, 5
        CONV_OPS = HALVES * TAPS
        TAIL_BANKS = 4
        RANK_OPS = 4
        RANK1_OPS = 3
        SOFT_OPS = 6

        def gate_cols(w, k, gate, quad):
            cols = w[:, k, gate * D:(gate + 1) * D] if k is not None else w[:, gate * D:(gate + 1) * D]
            return cols.rearrange("p (c q f) -> p c q f", c=HALVES, q=QUADS)[:, :, quad, :]

        def gate_out(ps, quad):
            return ps[QF * quad:QF * quad + B, 0:BLOCK].rearrange("p (c f) -> p c f", c=HALVES)

        def slot(buf, slots, i):
            return buf.rearrange("p (b c n) -> p c b n", c=HALVES, n=slots)[:, :, :, i]

        def hid_cols(i, k=None):
            h = slot(hid[i % 2][:, 2:2 + 3 * HB], 3, 0)
            return h if k is None else h[:, k, :]

        def turned_slot(buf, slots, i):
            return buf.rearrange("p (f c n) -> p c f n", c=HALVES, n=slots)[:, :, :, i]

        def halves_of(block):
            return block.rearrange("p (c f) -> p c f", c=HALVES)

        def step_slots(i, half):
            steps = cand_in[:, 0:STEPS * 4 * HB].rearrange("p (s b c n) -> p s b c n", s=STEPS, b=B, c=HALVES)
            return steps[:, :, :, half, i]

        def runs_after(n, least):
            return not isinstance(n, int) or n >= least

        FIRST_LOOP, LAST_LOOP = 3, CHUNKS - 2

        def iterations(eng, run):
            run(0, gru=True, pre=True, moe0=False, moe1=False)
            run(1, gru=True, pre=True, moe0=True, moe1=False)
            run(2, gru=True, pre=True, moe0=True, moe1=True)
            with eng.Fori(FIRST_LOOP, LAST_LOOP + 1) as c:
                run(c, gru=True, pre=True, moe0=True, moe1=True)
            run(CHUNKS - 1, gru=True, pre=False, moe0=True, moe1=True)
            run(CHUNKS, gru=False, pre=False, moe0=True, moe1=True)
            run(CHUNKS + 1, gru=False, pre=False, moe0=False, moe1=True)

        def turn_at(gru):
            return 3 if gru else 5

        def down_at(gru):
            return 5 if gru else 8

        TAIL_STEPS = 3 * (UNITS - 1) + down_at(False) + 1

        def gu_bank(u, gru):
            return ps_gu if gru else (ps_gu, ps_z, ps_r, ps_hn)[u % TAIL_BANKS]

        def moe1_step(s, moe0, gru):
            return s - 6 if moe0 and not gru else s

        def turned_bank(u, gru):
            return ps_t if gru or u % 2 == 0 else ps_gi

        def rank0_at(gru):
            return 2 if gru else 1

        def unit_of(s, at):
            u, rest = divmod(s - at, 3)
            return u if rest == 0 and 0 <= u < UNITS else None

        block = ctx.enter_context(nc.Block())

        @block.sync
        def _(sp):
            sp.dma_start(small[:, :, :], small_d).then_inc(loaded_small, 16)
            sp.dma_start(z_bias_rows[:, :, :], bias_d).then_inc(loaded_small, 16)
            sp.dma_start(x_pre[:, :, :], x_c[0].rearrange("p (c t) -> p c t", c=HALVES)).then_inc(x_pre_loaded, 16)
            sp.dma_start(w_ih[:, :, 0:2 * D], w_ih_d[:, :, 0:2 * D]).then_inc(loaded_in_rz, 16)
            sp.dma_start(w_ih[:, :, 2 * D:G3], w_ih_d[:, :, 2 * D:G3]).then_inc(loaded_in_n, 16)
            sp.dma_start(w_hh[:, :, :], w_hh_d).then_inc(loaded_gru, 16)

            def run(c, gru, pre, moe0, moe1):
                if pre:
                    sp.wait_ge(in_summed, c + 1)
                    sp.dma_start(x_pre[:, :, :], x_c[c + 1].rearrange("p (c t) -> p c t", c=HALVES))\
                      .then_inc(x_pre_loaded, 16)
                if isinstance(c, int) and c == 0:
                    sp.dma_start(gate_up[:, 1:UNITS, :, :], gu_d).then_inc(loaded_moe, 16)
                    sp.dma_start(down[:, 1:UNITS, :], dn_d).then_inc(loaded_moe, 16)
                    sp.dma_start(router0[:, :, :], r0_d).then_inc(loaded_moe, 16)
                    sp.dma_start(gate_up[:, 0, :, 0:I0], sg_d).then_inc(loaded_moe, 16)
                    sp.dma_start(gate_up[:, 0, :, I0:2 * I0], su_d).then_inc(loaded_moe, 16)
                    sp.dma_start(down[:, 0, :], sd_d).then_inc(loaded_moe, 16)
                    sp.dma_start(proj1[:, :, 0:E1 * I1], d1_d).then_inc(loaded_moe, 16)
                    sp.dma_start(proj1[:, :, E1 * I1:E1 * I1 + E1], r1_d).then_inc(loaded_moe, 16)
                    sp.dma_start(up1[:, :], u1_d).then_inc(loaded_moe, 16)
                if moe0:
                    if runs_after(c, 2):
                        sp.wait_ge(x1_ready, c - 1)
                    sp.dma_start(x_res[:, :, :], x_c[c - 1].rearrange("p (c t) -> p c t", c=HALVES))\
                      .then_inc(x_res_loaded, 16)
                if moe1:
                    sp.wait_ge(out_ready, c - 1)
                    sp.dma_start(out_c[c - 2].rearrange("p (c t) -> p c t", c=HALVES), out_sb[:, :, :])\
                      .then_inc(stored, 16)

            iterations(sp, run)
            sp.wait_ge(stored, 16 * CHUNKS)

        @block.gpsimd
        def _(pool):
            nc.gpsimd.memset(ident[:, :], 0.0).then_inc(pool_const, 1)
            nc.gpsimd.memset(before[:, :, :], 1.0).then_inc(pool_const, 1)
            nc.gpsimd.memset(ones[:, :, :], 1.0).then_inc(pool_const, 1)
            pool.wait_ge(pool_const, 3)
            nc.gpsimd.affine_select(out=ident[:, :], in_=ident[:, :], compare_op=ALU.not_equal, fill=1.0, base=0,
                                    pattern=[[-1, P]], channel_multiplier=1).then_inc(pool_const, 1)
            nc.gpsimd.affine_select(out=before[:, :, :], in_=before[:, :, :], compare_op=ALU.is_gt, fill=0.0, base=0,
                                    pattern=[[1, E0], [-1, E0]], channel_multiplier=0).then_inc(pool_const, 1)

            def run(c, gru, pre, moe0, moe1):
                if not gru:
                    return
                for s in range(STEPS):
                    pool.wait_ge(h_ready, STEPS * c + s + 2)
                    nc.gpsimd.tensor_tensor(hist[:, :, B * s:B * s + B], hid_cols(s + 1), ones[:, :, 0:B], ALU.mult)\
                      .then_inc(hist_kept, 1)
                if isinstance(c, int) and c == CHUNKS - 1:
                    return
                if runs_after(c, 1):
                    pool.wait_ge(gu_summed, UNITS * c)
                pool.wait_ge(hist_kept, STEPS * (c + 1))
                nc.gpsimd.tensor_tensor(moe0_x[:, :, :], hist[:, :, :], ones[:, :, :], ALU.mult)\
                  .then_inc(moe0_x_ready, 1)
                pool.wait_ge(moe0_x_ready, c + 1)

            iterations(pool, run)

        @block.scalar
        def _(act):
            def copy_gi_z(q):
                act.wait_ge(gi_summed, q + 1)
                if runs_after(q, 1):
                    act.wait_ge(gi_used, q)
                nc.scalar.activation(gi_z[:, :], ps_gi[:, 0:D], ACT.Copy).then_inc(gi_z_ready, 1)

            def place_gi_r(q):
                for half in range(HALVES):
                    nc.scalar.activation(
                        gi_r[:, half, :, :],
                        ps_gi[:, D + half * P:D + (half + 1) * P].rearrange("p (s b) -> p s b", b=B),
                        ACT.Identity, bias=r_bias[:, half:half + 1]).then_inc(gi_r_ready, 1)

            def place_in(q):
                act.wait_ge(in_summed, q + 1)
                for half in range(HALVES):
                    nc.scalar.activation(step_slots(2, half),
                                         ps_moe1[:, half * P:(half + 1) * P].rearrange("p (s b) -> p s b", b=B),
                                         ACT.Identity, bias=b_in[:, half:half + 1]).then_inc(in_ready, 1)

            act.wait_ge(biases_ready, BIASES)
            nc.scalar.activation(table_warm[:, :], b_in[:, 0:1], ACT.Sigmoid)
            copy_gi_z(0)
            place_gi_r(0)
            place_in(0)

            def gru_step(c, s):
                n = STEPS * c + s
                act.wait_ge(r_arg_ready, n + 1)
                nc.scalar.activation(slot(cand_mul[:, :], 4, 2), r_arg[:, :, :], ACT.Sigmoid).then_inc(cand_parts, 1)
                act.wait_ge(z_summed, n + 1)
                nc.scalar.activation(z_rows[:, :], ps_z[:, 0:BLOCK], ACT.Sigmoid).then_inc(z_rows_ready, 1)
                act.wait_ge(arg_ready, n + 1)
                four_in = cand_out[:, :].rearrange("p (j four) -> p j four", four=4)[:, :, 2:4]
                trip_out = hid[s % 2][:, 2:2 + 3 * HB].rearrange("p (j three) -> p j three", three=3)[:, :, 1:3]
                nc.scalar.activation(trip_out, four_in, ACT.Tanh, scale=-1.0).then_inc(upd_parts, 1)

            def run(c, gru, pre, moe0, moe1):
                for s in range(STEPS if gru else TAIL_STEPS):
                    if gru:
                        gru_step(c, s)
                    if moe0:
                        q = c - 1
                        if s == rank0_at(gru):
                            act.wait_ge(logits0_ready, q + 1)
                            nc.scalar.activation(sig0[:, :], logits0[:, :], ACT.Sigmoid).then_inc(sig0_ready, 1)
                        u = unit_of(s, 1)
                        if u is not None:
                            n = UNITS * q + u
                            act.wait_ge(gu_summed, n + 1)
                            left = n if gru or u == 0 else n - 1
                            if runs_after(left, 1):
                                act.wait_ge(hidden0_ready, left)
                            if u == 0:
                                nc.scalar.activation(sig_gate[u % 2][:, :], gu_bank(u, gru)[:, 0:I0], ACT.Sigmoid)\
                                  .then_inc(sig_gate_ready, 1)
                            else:
                                if u == 1:
                                    act.wait_ge(rank0_step, RANK_OPS * (q + 1))
                                nc.scalar.activation(sig_gate[u % 2][:, :], gu_bank(u, gru)[:, 0:I0], ACT.Sigmoid,
                                                     scale=probs[:, u - 1:u]).then_inc(sig_gate_ready, 1)
                        u = unit_of(s, turn_at(gru))
                        if u is not None:
                            n = UNITS * q + u
                            act.wait_ge(hidden0_turned, n + 1)
                            free = n if gru or u == 0 else n - 1
                            if runs_after(free, 1):
                                act.wait_ge(down_summed, free)
                            nc.scalar.activation(hidden0_c[u % 2][:, :], turned_bank(u, gru)[:, 0:P], ACT.Copy)\
                              .then_inc(hidden0_c_ready, 1)
                    if moe1:
                        q = c - 2
                        step = moe1_step(s, moe0, gru)
                        if step == 13:
                            act.wait_ge(top1_ready, 2 * (q + 1))
                            nc.scalar.activation(sig_up[:, :], ps_moe1[:, E1 * I1:E1 * I1 + E1], ACT.Sigmoid,
                                                 bias=neg_top1[:, 0:1]).then_inc(exp_ready, 1)
                            nc.scalar.activation(sig_dn[:, :], ps_moe1[:, E1 * I1:E1 * I1 + E1], ACT.Sigmoid,
                                                 bias=top1[:, 0:1], scale=-1.0).then_inc(exp_ready, 1)
                            nc.scalar.activation(sig_hx[:, :], ps_moe1[:, 0:E1 * I1], ACT.Sigmoid)\
                              .then_inc(sig_hx_ready, 1)
                        if step == 19:
                            act.wait_ge(gated1_turned, q + 1)
                            nc.scalar.activation(gated1_c[:, :], ps_moe1[:, D:D + P], ACT.Copy)\
                              .then_inc(gated1_c_ready, 1)
                    if pre:
                        if s == STEPS - 2:
                            copy_gi_z(c + 1)
                        if s == STEPS - 1:
                            place_gi_r(c + 1)
                            place_in(c + 1)

            iterations(act, run)

        @block.vector
        def _(dve):
            for part in (ps_r[:, 0:BLOCK], ps_hn[:, 0:BLOCK], ps_z[:, 0:BLOCK], cand_mul[:, :],
                         upd_mul[:, 0:3 * HB], hid[0][:, :], hid[1][:, :], x1[:, :, 0:CARRY]):
                nc.vector.memset(part, 0.0).then_inc(cleared, 1)
            for half in range(HALVES):
                nc.vector.memset(step_slots(3, half), 0.0).then_inc(cleared, 1)
            dve.wait_ge(loaded_small, 16 * SMALL_LOADS)
            nc.vector.tensor_tensor(z_bias[:, :], z_bias_rows[:, 0, :], z_bias_rows[:, 1, :], ALU.add)\
              .then_inc(biases_ready, 1)
            nc.vector.tensor_tensor(r_bias[:, :], b_ir, b_hr, ALU.add).then_inc(biases_ready, 1)
            dve.wait_ge(cleared, CLEARS)
            nc.vector.memset(slot(cand_mul[:, :], 4, 1), 1.0).then_inc(masks_ready, 1)
            nc.vector.memset(slot(cand_mul[:, :], 4, 3), -1.0).then_inc(masks_ready, 1)
            nc.vector.memset(slot(upd_mul[:, 0:3 * HB], 3, 1), 1.0).then_inc(masks_ready, 1)
            nc.vector.tensor_copy(hid_cols(0), cond).then_inc(h_ready, 1)
            for half in range(HALVES):
                nc.vector.tensor_copy(step_slots(0, half), b_hn[:, half:half + 1, None].to_broadcast([P, STEPS, B]))\
                  .then_inc(biases_ready, 1)
            dve.wait_ge(biases_ready, BIASES)
            dve.wait_ge(masks_ready, 3)
            dve.wait_ge(pool_const, POOL_CONSTS)

            def turn_rh(c, n, s):
                dve.wait_ge(r_summed, n + 1)
                nc.vector.transpose(turned_r[:, :], ps_r[:, 0:BLOCK]).then_inc(r_turned, 1)
                dve.wait_ge(r_turned, n + 1)
                if s == 0:
                    dve.wait_ge(gi_r_ready, HALVES * (c + 1))
                nc.vector.tensor_tensor(r_arg[:, :, :], halves_of(turned_r[:, :])[:, :, 0:B], gi_r[:, :, s, :],
                                        ALU.add)\
                  .then_inc(r_arg_ready, 1)
                dve.wait_ge(hn_summed, n + 1)
                nc.vector.transpose(turned_slot(cand_in[:, 4 * HB * s:4 * HB * s + 4 * BLOCK], 4, 1),
                                    halves_of(ps_hn[:, 0:BLOCK])).then_inc(cand_parts, 1)

            def candidate(c, n, s):
                dve.wait_ge(cand_parts, 2 * (n + 1))
                if s == 0:
                    dve.wait_ge(in_ready, HALVES * (c + 1))
                nc.vector.tensor_tensor_scan(cand_out[:, :], cand_mul[:, :], cand_in[:, 4 * HB * s:4 * HB * (s + 1)],
                                             0.0, ALU.mult, ALU.add).then_inc(arg_ready, 1)

            def turn_z(n):
                dve.wait_ge(z_rows_ready, n + 1)
                nc.vector.transpose(turned_slot(upd_mul[:, :], 3, 2), halves_of(z_rows[:, :])).then_inc(upd_parts, 1)

            def update(n, s):
                dve.wait_ge(upd_parts, 2 * (n + 1))
                if runs_after(n, 2):
                    dve.wait_ge(hist_kept, n - 1)
                nc.vector.tensor_tensor_scan(hid[(s + 1) % 2][:, 0:3 * HB], upd_mul[:, 0:3 * HB],
                                             hid[s % 2][:, 2:2 + 3 * HB], 0.0, ALU.mult, ALU.add).then_inc(h_ready, 1)

            def compare(values, which, op):
                at_j = values[:, None, :].to_broadcast([P, E0, E0])
                at_e = values[:, :, None].to_broadcast([P, E0, E0])
                return nc.vector.tensor_tensor(pairs[:, :, which, :], at_j, at_e, op)

            def unit_hidden(q, u, gru):
                n = UNITS * q + u
                ps_unit, sig, act_g, hidden = gu_bank(u, gru), sig_gate[u % 2], act_gate[u % 2], hidden0[u % 2]
                dve.wait_ge(sig_gate_ready, n + 1)
                if u == 0:
                    nc.vector.tensor_tensor(act_g[:, :], ps_unit[:, 0:I0], sig[:, :], ALU.mult)\
                      .then_inc(act_gate_ready, 1)
                else:
                    nc.vector.scalar_tensor_tensor(act_g[:, :], ps_unit[:, 0:I0], probs[:, u - 1:u], sig[:, :],
                                                   ALU.mult, ALU.mult).then_inc(act_gate_ready, 1)
                dve.wait_ge(act_gate_ready, n + 1)
                turned_units = n if gru or u == 0 else n - 1
                if runs_after(turned_units, 1):
                    dve.wait_ge(hidden0_turned, turned_units)
                if u == 0:
                    nc.vector.tensor_tensor(hidden[:, :], ps_unit[:, I0:2 * I0], act_g[:, :], ALU.mult)\
                      .then_inc(hidden0_ready, 1)
                else:
                    nc.vector.scalar_tensor_tensor(hidden[:, :], ps_unit[:, I0:2 * I0], probs[:, u - 1:u],
                                                   act_g[:, :], ALU.mult, ALU.mult).then_inc(hidden0_ready, 1)

            def moe0_part(q, s, gru):
                if s == rank0_at(gru):
                    dve.wait_ge(logits0_summed, q + 1)
                    nc.vector.tensor_copy(logits0[:, :], ps_t[:, 0:E0]).then_inc(logits0_ready, 1)
                if s == rank0_at(gru) + 1:
                    dve.wait_ge(logits0_ready, q + 1)
                    compare(logits0, 0, ALU.is_gt)
                    compare(logits0, 1, ALU.is_equal).then_inc(rank0_step, 1)
                    dve.wait_ge(rank0_step, RANK_OPS * q + 1)
                    nc.vector.tensor_tensor(pairs[:, :, 1, :], pairs[:, :, 1, :], before[:, :, :], ALU.mult)\
                      .then_inc(rank0_step, 1)
                if s == rank0_at(gru) + (2 if gru else 1):
                    dve.wait_ge(rank0_step, RANK_OPS * q + 2)
                    nc.vector.tensor_reduce(rank[:, :], pairs[:, :, :, :], AX.XY, ALU.add).then_inc(rank0_step, 1)
                    dve.wait_ge(rank0_step, RANK_OPS * q + 3)
                    dve.wait_ge(sig0_ready, q + 1)
                    nc.vector.scalar_tensor_tensor(probs[:, :], rank[:, :], 1.5, sig0[:, :], ALU.is_lt, ALU.mult)\
                      .then_inc(rank0_step, 1)
                u = unit_of(s, 2)
                if u is not None:
                    unit_hidden(q, u, gru)
                if s == (STEPS - 2 if gru else TAIL_STEPS - 1):
                    dve.wait_ge(down_summed, UNITS * (q + 1))
                    dve.wait_ge(x_res_loaded, 16 * (q + 1))
                    if runs_after(q, 1):
                        dve.wait_ge(carried, q)
                    nc.vector.tensor_tensor(x1[:, :, CARRY:CARRY + P],
                                            ps_moe0[:, 0:D].rearrange("p (c t) -> p c t", c=HALVES), x_res[:, :, :],
                                            ALU.add).then_inc(x1_ready, 1)

            def conv(q, tap):
                for half in range(HALVES):
                    src = x1[:, half, B * tap:B * tap + P]
                    w = cond[:, half, tap:tap + 1]
                    if tap == 0:
                        if runs_after(q, 1):
                            dve.wait_ge(proj1_summed, q)
                        nc.vector.tensor_scalar(y[:, half, :], src, w, conv_b[:, half:half + 1], ALU.mult, ALU.add)\
                          .then_inc(conv_step, 1)
                    else:
                        dve.wait_ge(conv_step, CONV_OPS * q + HALVES * (tap - 1) + half + 1)
                        nc.vector.scalar_tensor_tensor(y[:, half, :], src, w, y[:, half, :], ALU.mult, ALU.add)\
                          .then_inc(conv_step, 1)

            def moe1_part(q, s):
                if s == 0:
                    dve.wait_ge(x1_ready, q + 1)
                if s in (0, 1, 6, 7):
                    conv(q, (0, 1, 6, 7).index(s))
                if s == 12:
                    dve.wait_ge(proj1_summed, q + 1)
                    nc.vector.tensor_reduce(top1[:, :], ps_moe1[:, E1 * I1:E1 * I1 + E1], AX.X, ALU.max)\
                      .then_inc(top1_ready, 1)
                    nc.vector.tensor_copy(logits1[:, :], ps_moe1[:, E1 * I1:E1 * I1 + E1]).then_inc(logits1_ready, 1)
                    dve.wait_ge(top1_ready, 2 * q + 1)
                    nc.vector.tensor_scalar(neg_top1[:, :], top1[:, :], -1.0, None, ALU.mult).then_inc(top1_ready, 1)
                    dve.wait_ge(logits1_ready, q + 1)
                    compare(logits1, 0, ALU.is_gt)
                if s == 13:
                    compare(logits1, 1, ALU.is_equal).then_inc(rank1_step, 1)
                    dve.wait_ge(rank1_step, RANK1_OPS * q + 1)
                    nc.vector.tensor_tensor(pairs[:, :, 1, :], pairs[:, :, 1, :], before[:, :, :], ALU.mult)\
                      .then_inc(rank1_step, 1)
                if s == 15:
                    dve.wait_ge(exp_ready, 2 * (q + 1))
                    nc.vector.reciprocal(sig_dn[:, :], sig_dn[:, :]).then_inc(soft_step, 1)
                    dve.wait_ge(rank1_step, RANK1_OPS * q + 2)
                    nc.vector.tensor_reduce(rank[:, :], pairs[:, :, :, :], AX.XY, ALU.add).then_inc(rank1_step, 1)
                    dve.wait_ge(soft_step, SOFT_OPS * q + 1)
                    nc.vector.tensor_tensor(expd[:, :], sig_up[:, :], sig_dn[:, :], ALU.mult).then_inc(soft_step, 1)
                    dve.wait_ge(soft_step, SOFT_OPS * q + 2)
                    nc.vector.tensor_reduce(total[:, :], expd[:, :], AX.X, ALU.add).then_inc(soft_step, 1)
                if s == 16:
                    dve.wait_ge(rank1_step, RANK1_OPS * (q + 1))
                    nc.vector.scalar_tensor_tensor(chosen[:, :], rank[:, :], 1.5, expd[:, :], ALU.is_lt, ALU.mult)\
                      .then_inc(soft_step, 1)
                    dve.wait_ge(soft_step, SOFT_OPS * q + 3)
                    nc.vector.reciprocal(total[:, :], total[:, :]).then_inc(soft_step, 1)
                    dve.wait_ge(sig_hx_ready, q + 1)
                    nc.vector.tensor_tensor(act1[:, :], ps_moe1[:, 0:E1 * I1], sig_hx[:, :], ALU.mult)\
                      .then_inc(act1_ready, 1)
                    dve.wait_ge(soft_step, SOFT_OPS * q + 5)
                    nc.vector.tensor_scalar(gate1[:, :], chosen[:, :], total[:, 0:1], None, ALU.mult)\
                      .then_inc(soft_step, 1)
                if s == 18:
                    dve.wait_ge(act1_ready, q + 1)
                    dve.wait_ge(soft_step, SOFT_OPS * (q + 1))
                    nc.vector.tensor_tensor(gated1[:, :].rearrange("p (e i) -> p e i", e=E1),
                                            act1[:, :].rearrange("p (e i) -> p e i", e=E1),
                                            gate1[:, :, None].to_broadcast([P, E1, I1]), ALU.mult)\
                      .then_inc(gated1_ready, 1)
                if s == 24:
                    dve.wait_ge(moe1_summed, q + 1)
                    if runs_after(q, 1):
                        dve.wait_ge(stored, 16 * q)
                    nc.vector.tensor_tensor(out_sb[:, :, :], ps_moe1[:, 0:D].rearrange("p (c t) -> p c t", c=HALVES),
                                            x1[:, :, CARRY:CARRY + P], ALU.add).then_inc(out_ready, 1)
                if s == 25:
                    nc.vector.tensor_copy(x1[:, :, 0:CARRY], x1[:, :, P:P + CARRY]).then_inc(carried, 1)

            def run(c, gru, pre, moe0, moe1):
                for s in range(STEPS if gru else TAIL_STEPS):
                    if gru:
                        n = STEPS * c + s
                        turn_rh(c, n, s)
                        candidate(c, n, s)
                        turn_z(n)
                        update(n, s)
                    if moe0:
                        moe0_part(c - 1, s, gru)
                    if moe1:
                        moe1_part(c - 2, moe1_step(s, moe0, gru))

            iterations(dve, run)

        @block.tensor
        def _(pe):
            def input_z(q, s):
                n = STEPS * q + s
                if s == 0:
                    pe.wait_ge(gi_z_ready, q + 1)
                if runs_after(n, 1):
                    pe.wait_ge(z_rows_ready, n)
                for quad in range(QUADS):
                    last = nc.tensor.matmul(gate_out(ps_z, quad), ident[:, B * s:B * s + B],
                                            gate_cols(gi_z, None, 0, quad), start=True, stop=False,
                                            skip_group_check=True)
                if s == STEPS - 1:
                    last.then_inc(gi_used, 1)

            def gru_step(c, s):
                n = STEPS * c + s
                pe.wait_ge(h_ready, n + 1)
                for ps, gate, summed in ((ps_r, 0, r_summed), (ps_hn, 2, hn_summed), (ps_z, 1, z_summed)):
                    for k in range(HALVES):
                        for quad in range(QUADS):
                            last = nc.tensor.matmul(gate_out(ps, quad), hid_cols(s, k), gate_cols(w_hh, k, gate, quad),
                                                    start=(gate != 1 and k == 0), stop=(k == HALVES - 1),
                                                    skip_group_check=True)
                    last.then_inc(summed, 1)

            COLS = D // P
            PRE_PARTS = COLS + HALVES * COLS + HALVES * HALVES

            def pre_rz(q, j):
                if j == 0:
                    if runs_after(q, 1):
                        pe.wait_ge(gi_z_ready, q)
                        pe.wait_ge(gi_r_ready, HALVES * q)
                if j == COLS:
                    pe.wait_ge(x_pre_loaded, 16 * (q + 1))
                k, col = j // COLS - 1, j % COLS
                if k < 0:
                    nc.tensor.matmul(ps_gi[:, P * col:P * (col + 1)], ones[0:1, 0, :],
                                     z_bias[0:1, P * col:P * (col + 1)], start=(col == 0), stop=False,
                                     skip_group_check=True)
                elif k < HALVES:
                    nc.tensor.matmul(ps_gi[:, P * col:P * (col + 1)], x_pre[:, k, :],
                                     w_ih[:, k, D + P * col:D + P * (col + 1)], start=False, stop=(k == HALVES - 1),
                                     skip_group_check=True)
                else:
                    half, k = divmod(j - COLS - HALVES * COLS, HALVES)
                    last = nc.tensor.matmul(ps_gi[:, D + half * P:D + (half + 1) * P],
                                            w_ih[:, k, half * P:(half + 1) * P], x_pre[:, k, :], start=False,
                                            stop=(k == HALVES - 1), skip_group_check=True)
                if j == PRE_PARTS - 1:
                    last.then_inc(gi_summed, 1)

            def pre_in(q, j, moe1_done):
                half, k = j // HALVES, j % HALVES
                if j == 0:
                    if runs_after(q, 1):
                        pe.wait_ge(in_ready, HALVES * q)
                    if moe1_done is not None:
                        pe.wait_ge(out_ready, moe1_done)
                last = nc.tensor.matmul(ps_moe1[:, half * P:(half + 1) * P],
                                        w_ih[:, k, 2 * D + half * P:2 * D + (half + 1) * P], x_pre[:, k, :],
                                        start=(j == 0), stop=(k == HALVES - 1), skip_group_check=True)
                if j == 2 * HALVES - 1:
                    last.then_inc(in_summed, 1)

            def moe0_logits(q, x):
                if runs_after(q, 1):
                    pe.wait_ge(hidden0_c_ready, UNITS * q)
                for k in range(HALVES):
                    last = nc.tensor.matmul(ps_t[:, 0:E0], x[:, k, :], router0[:, k, :], start=(k == 0),
                                            stop=(k == HALVES - 1))
                last.then_inc(logits0_summed, 1)

            def moe0_part(q, s, gru):
                x = moe0_x if gru else hist
                if s == 0 and gru:
                    pe.wait_ge(moe0_x_ready, q + 1)
                elif s == 0:
                    pe.wait_ge(hist_kept, T)
                    moe0_logits(q, x)
                u = unit_of(s, 0)
                if u is not None:
                    n = UNITS * q + u - (0 if gru else TAIL_BANKS - 1)
                    if runs_after(n, 1):
                        pe.wait_ge(hidden0_ready, n)
                    nc.tensor.matmul(gu_bank(u, gru)[:, 0:2 * I0], x[:, 0, :], gate_up[:, u, 0, :], start=True,
                                     stop=False)
                u = unit_of(s, 1)
                if u is not None:
                    last = nc.tensor.matmul(gu_bank(u, gru)[:, 0:2 * I0], x[:, 1, :], gate_up[:, u, 1, :],
                                            start=False, stop=True)
                    last.then_inc(gu_summed, 1)
                if s == 2 and gru:
                    moe0_logits(q, x)
                u = unit_of(s, turn_at(gru))
                if u is not None:
                    n = UNITS * q + u
                    pe.wait_ge(hidden0_ready, n + 1)
                    if u == 0:
                        pe.wait_ge(logits0_ready, q + 1)
                    else:
                        pe.wait_ge(hidden0_c_ready, n if gru else n - 1)
                    nc.tensor.transpose(turned_bank(u, gru)[:, 0:P], hidden0[u % 2][:, :], ident[:, :])\
                      .then_inc(hidden0_turned, 1)
                u = unit_of(s, down_at(gru))
                if u is not None:
                    n = UNITS * q + u
                    pe.wait_ge(hidden0_c_ready, n + 1)
                    if u == 0 and runs_after(q, 1):
                        pe.wait_ge(x1_ready, q)
                    for half in range(HALVES):
                        last = nc.tensor.matmul(ps_moe0[:, half * P:(half + 1) * P],
                                                down[:, u, half * P:(half + 1) * P], hidden0_c[u % 2][:, :],
                                                start=(u == 0 and half == 0), stop=(u == UNITS - 1),
                                                skip_group_check=True)
                    last.then_inc(down_summed, 1)

            def moe1_part(q, s):
                if s in (8, 10):
                    k = (8, 10).index(s)
                    if k == 0:
                        pe.wait_ge(conv_step, CONV_OPS * (q + 1))
                        placed = min(q + 3, CHUNKS) if isinstance(q, int) else q + 3
                        pe.wait_ge(in_ready, HALVES * placed)
                        if runs_after(q, 1):
                            pe.wait_ge(out_ready, q)
                    last = nc.tensor.matmul(ps_moe1[:, 0:E1 * I1 + E1], y[:, k, :], proj1[:, k, :], start=(k == 0),
                                            stop=(k == HALVES - 1))
                    if k == HALVES - 1:
                        last.then_inc(proj1_summed, 1)
                if s == 19:
                    pe.wait_ge(gated1_ready, q + 1)
                    nc.tensor.transpose(ps_moe1[:, D:D + P], gated1[:, :], ident[:, :]).then_inc(gated1_turned, 1)
                if s in (20, 22):
                    half = (20, 22).index(s)
                    if half == 0:
                        pe.wait_ge(gated1_c_ready, q + 1)
                    last = nc.tensor.matmul(ps_moe1[:, half * P:(half + 1) * P], up1[:, half * P:(half + 1) * P],
                                            gated1_c[:, :], start=(half == 0), stop=True, skip_group_check=True)
                    if half == HALVES - 1:
                        last.then_inc(moe1_summed, 1)

            RZ_AT = (1, 2, 4, 5, 7, 11, 13, 14, 16, 17)
            IN_AT = (27, 27, 28, 28)

            def pre_part(q, s, moe1_done):
                for j, at in enumerate(RZ_AT):
                    if at == s:
                        pre_rz(q, j)
                for j, at in enumerate(IN_AT):
                    if at == s:
                        pre_in(q, j, moe1_done)

            LONE_WARM_UPS = {7: 6, 18: 7}

            def keep_warm(blocks=2, bank=ps_gu):
                nc.tensor.matmul(bank[:, 0:P * blocks], ident[:, :], ones[:, 0:blocks, :], start=True, stop=True)

            def run(c, gru, pre, moe0, moe1):
                if isinstance(c, int) and c == 1:
                    pe.wait_ge(loaded_moe, 16 * MOE_LOADS)
                for s in range(STEPS if gru else TAIL_STEPS):
                    if gru:
                        gru_step(c, s)
                    if moe0:
                        moe0_part(c - 1, s, gru)
                    if moe1:
                        moe1_part(c - 2, moe1_step(s, moe0, gru))
                    if pre:
                        pre_part(c + 1, s, c - 1 if moe1 else None)
                    if gru and (moe0 or s not in IN_AT) and (s >= STEPS - 2 or not moe0):
                        keep_warm()
                    elif gru and not pre and (s in RZ_AT or s in IN_AT):
                        pe.wait_ge(gi_r_ready, HALVES * CHUNKS)
                        keep_warm(1, ps_gi)
                    if not moe0 and not gru and s in LONE_WARM_UPS:
                        for _ in range(LONE_WARM_UPS[s]):
                            keep_warm()
                    if gru and s < STEPS - 1:
                        input_z(c, s + 1)
                    elif pre:
                        input_z(c + 1, 0)

            pe.wait_ge(pool_const, POOL_CONSTS)
            for _ in range(WARM_UPS):
                keep_warm()
            pe.wait_ge(biases_ready, BIASES)
            pe.wait_ge(cleared, CLEARS)
            for j in range(COLS):
                pre_rz(0, j)
            pe.wait_ge(loaded_in_rz, 16)
            for j in range(COLS, PRE_PARTS):
                pre_rz(0, j)
            pe.wait_ge(loaded_in_n, 16)
            for j in range(2 * HALVES):
                pre_in(0, j, None)
            input_z(0, 0)
            pe.wait_ge(loaded_gru, 16)
            iterations(pe, run)


def kernel(x, cond_2048, L0_cond_W_ih, L0_cond_W_hh, L0_cond_b_ih, L0_cond_b_hh, L0_ffn_router_w, L0_ffn_gate_up_w,
           L0_ffn_down_w, L0_ffn_shared_gate_w, L0_ffn_shared_up_w, L0_ffn_shared_down_w, L1_cond_b, L1_ffn_router_w,
           L1_ffn_down_w, L1_ffn_up_w):
    import numpy as np
    import concourse.bacc as bacc
    from concourse.bass_utils import run_bass_kernel_spmd

    def halves(w):
        w = np.asarray(w)
        return w.reshape((HALVES, P) + w.shape[1:]).swapaxes(0, 1)

    chunked = np.asarray(x).reshape(B, CHUNKS, STEPS, HALVES, P).transpose(1, 4, 3, 2, 0)
    arrays = {
        "x_c": chunked.reshape(CHUNKS, P, D),
        "small": np.concatenate([halves(np.asarray(cond_2048).T)] + [halves(np.asarray(v))[:, :, None] for v in (
            L0_cond_b_ih[2 * D:], L0_cond_b_hh[2 * D:], L1_cond_b, L0_cond_b_ih[:D], L0_cond_b_hh[:D])], axis=2),
        "bias": np.stack([np.asarray(L0_cond_b_ih)[D:2 * D], np.asarray(L0_cond_b_hh)[D:2 * D]])[None],
        "w_ih": halves(L0_cond_W_ih),
        "w_hh": halves(L0_cond_W_hh),
        "r0": halves(L0_ffn_router_w),
        "gu": np.asarray(L0_ffn_gate_up_w).reshape(E0, HALVES, P, 2 * I0).transpose(2, 0, 1, 3),
        "dn": np.asarray(L0_ffn_down_w).transpose(1, 0, 2),
        "sg": halves(L0_ffn_shared_gate_w),
        "su": halves(L0_ffn_shared_up_w),
        "sd": np.asarray(L0_ffn_shared_down_w),
        "r1": halves(np.asarray(L1_ffn_router_w).T),
        "d1": halves(np.asarray(L1_ffn_down_w).transpose(2, 0, 1).reshape(D, E1 * I1)),
        "u1": np.asarray(L1_ffn_up_w).transpose(0, 2, 1).reshape(E1 * I1, D),
    }
    arrays = {f"in_{name}": np.ascontiguousarray(a) for name, a in arrays.items()}
    nc = bacc.Bacc("TRN2", target_bir_lowering=False, num_devices=1)
    args = [nc.dram_tensor(name, a.shape, mybir.dt.from_np(a.dtype), kind="ExternalInput").ap()
            for name, a in arrays.items()]
    out = nc.dram_tensor("out_c", (CHUNKS, P, D), F32, kind="ExternalOutput").ap()
    build(nc, *args, out)
    got = run_bass_kernel_spmd(nc, [arrays], core_ids=[0]).results[0]["out_c"]
    return got.reshape(CHUNKS, P, HALVES, STEPS, B).transpose(4, 0, 3, 2, 1).reshape(B, T, D)
```
